# Optimizing a Trainium2 kernel written in Bass

```python
import numpy as np
import jax
import jax.numpy as jnp

def _softmax(x, axis=-1):
    return jax.nn.softmax(x, axis=axis)
def _gelu(x):
    return jax.nn.gelu(x, approximate=True)
def _silu(x):
    return jax.nn.silu(x)
def _sigmoid(x):
    return jax.nn.sigmoid(x)
def _layernorm(x, axis=-1, eps=1e-5):
    m = jnp.mean(x, axis=axis, keepdims=True)
    v = jnp.var(x, axis=axis, keepdims=True)
    return (x - m) / jnp.sqrt(v + eps)
def _scatter_add(tgt, idx, src, axis=0):
    return tgt.at[idx].add(src)
def _segment_sum(src, seg, n):
    return jax.ops.segment_sum(src, seg, n)

kernel_name = 'mk_adj_resnorm_d4_adj_128_c7d676'

def setup_inputs(seed: int = 0):
    np.random.seed(seed)
    _w = jnp.asarray
    def _rec_inputs():
        import jax
        import jax.numpy as jnp
        _gk = jax.random.key(seed)
        x = -0.000929 + 1 * jax.random.normal(jax.random.fold_in(_gk, 1), (2708, 128), jnp.float32)
        _a = jax.random.bernoulli(jax.random.fold_in(_gk, 2), 0.0014771, (2708, 2708))
        _a = jnp.logical_or(_a, jnp.swapaxes(_a, -1, -2))
        _a = jnp.logical_or(_a, jnp.eye(2708, dtype=bool))
        _af = _a.astype(jnp.float32)
        _af = _af * jax.random.uniform(jax.random.fold_in(_gk, 3), (2708, 2708), jnp.float32, 0.05, 1)
        adj = _af
        return x, adj
    x, adj = _rec_inputs()
    def _L0_gnn_setup():
        import jax, jax.numpy as jnp
        import numpy as np
        N = 8192
        F_IN = 128
        F_OUT = 128
        ALPHA = 0.2
        NEG_INF = -9000000000000000.0

        def _signed_adj(key, n, p=0.002):
            r = jax.random.uniform(key, (n, n), dtype=jnp.float32)
            return jnp.where(r < p, 1.0, jnp.where(r > 1.0 - p, -1.0, 0.0)).astype(jnp.float32)
        key = jax.random.key(seed)
        k_h, k_na, k_ea, k_w, k_a = jax.random.split(key, 5)
        h = jax.random.normal(k_h, (N, F_IN), dtype=jnp.float32)
        node_adj = _signed_adj(k_na, N)
        edge_adj = _signed_adj(k_ea, N)
        lim_w = 1.414 * np.sqrt(6.0 / (F_IN + F_OUT))
        W = jax.random.uniform(k_w, (F_IN, F_OUT), dtype=jnp.float32, minval=-lim_w, maxval=lim_w)
        lim_a = 1.414 * np.sqrt(6.0 / (2 * F_OUT + 1))
        a = jax.random.uniform(k_a, (2 * F_OUT, 1), dtype=jnp.float32, minval=-lim_a, maxval=lim_a)
        return {'h': h, 'node_adj': node_adj, 'edge_adj': edge_adj, 'W': W, 'a': a}
    _L0_gnn_all = _L0_gnn_setup()
    _L0_gnn_in = {k: v for k, v in _L0_gnn_all.items() if k in ('W', 'a', )}
    del _L0_gnn_all

    def _L1_gnn_setup():
        import jax, jax.numpy as jnp
        import numpy as np
        N = 8192
        IN_DIM = 128
        OUT_DIM = 128
        EDGE_P = 0.002
        key = jax.random.key(seed)
        k1, k2, k3, k4 = jax.random.split(key, 4)
        H = jax.random.normal(k1, (N, IN_DIM), dtype=jnp.float32)
        A = (jax.random.uniform(k2, (N, N)) < EDGE_P).astype(jnp.float32)
        limit = np.sqrt(6.0 / (IN_DIM + OUT_DIM)).astype(np.float32)
        W = jax.random.uniform(k3, (OUT_DIM, IN_DIM), minval=-limit, maxval=limit, dtype=jnp.float32)
        bound = 1.0 / np.sqrt(IN_DIM)
        b = jax.random.uniform(k4, (OUT_DIM,), minval=-bound, maxval=bound, dtype=jnp.float32)
        return {'H': H, 'A': A, 'W': W, 'b': b}
    _L1_gnn_all = _L1_gnn_setup()
    _L1_gnn_in = {k: v for k, v in _L1_gnn_all.items() if k in ('W', 'b', )}
    del _L1_gnn_all

    def _L2_gnn_setup():
        import jax, jax.numpy as jnp
        import numpy as np
        N, IN_DIM, OUT_DIM, HEADS = (4096, 128, 32, 4)
        EDGE_PROB = 0.015
        key = jax.random.key(seed)
        k1, k2, k3, k4 = jax.random.split(key, 4)
        x = jax.random.normal(k1, (N, IN_DIM), dtype=jnp.float32)
        adj = (jax.random.uniform(k2, (N, N)) < EDGE_PROB).astype(jnp.float32)
        adj = jnp.maximum(adj, jnp.eye(N, dtype=jnp.float32))
        W = jax.random.normal(k3, (IN_DIM, OUT_DIM * HEADS), dtype=jnp.float32) / np.sqrt(IN_DIM).astype(np.float32)
        a = jax.random.normal(k4, (2 * OUT_DIM,), dtype=jnp.float32) / np.sqrt(2 * OUT_DIM).astype(np.float32)
        return {'x': x, 'adj': adj, 'W': W, 'a': a}
    _L2_gnn_all = _L2_gnn_setup()
    _L2_gnn_in = {k: v for k, v in _L2_gnn_all.items() if k in ('W', 'a', )}
    del _L2_gnn_all

    def _L3_gnn_setup():
        import jax, jax.numpy as jnp
        import numpy as np
        LN_EPS = 1e-05
        key = jax.random.key(seed)
        ks = jax.random.split(key, 6)
        N, D = (1024, 128)
        return {'node_feats': jax.random.normal(ks[0], (N, D), dtype=jnp.float32), 'adj': jax.random.uniform(ks[1], (N, N), dtype=jnp.float32), 'msg_w': jax.random.normal(ks[2], (D, 2 * D), dtype=jnp.float32) * 0.05, 'msg_b': jax.random.normal(ks[3], (D,), dtype=jnp.float32) * 0.05, 'upd_w': jax.random.normal(ks[4], (D, 2 * D), dtype=jnp.float32) * 0.05, 'upd_b': jax.random.normal(ks[5], (D,), dtype=jnp.float32) * 0.05, 'ln_w': jnp.ones((D,), dtype=jnp.float32), 'ln_b': jnp.zeros((D,), dtype=jnp.float32)}
    _L3_gnn_all = _L3_gnn_setup()
    _L3_gnn_in = {k: v for k, v in _L3_gnn_all.items() if k in ('msg_w', 'msg_b', 'upd_w', 'upd_b', 'ln_w', 'ln_b', )}
    del _L3_gnn_all

    return {
        "x": x,
        "adj": adj,
        "L0_gnn_W": _L0_gnn_in["W"],
        "L0_gnn_a": _L0_gnn_in["a"],
        "L1_gnn_W": _L1_gnn_in["W"],
        "L1_gnn_b": _L1_gnn_in["b"],
        "L2_gnn_W": _L2_gnn_in["W"],
        "L2_gnn_a": _L2_gnn_in["a"],
        "L3_gnn_msg_w": _L3_gnn_in["msg_w"],
        "L3_gnn_msg_b": _L3_gnn_in["msg_b"],
        "L3_gnn_upd_w": _L3_gnn_in["upd_w"],
        "L3_gnn_upd_b": _L3_gnn_in["upd_b"],
        "L3_gnn_ln_w": _L3_gnn_in["ln_w"],
        "L3_gnn_ln_b": _L3_gnn_in["ln_b"],
    }

def reference(x, adj, L0_gnn_W, L0_gnn_a, L1_gnn_W, L1_gnn_b, L2_gnn_W, L2_gnn_a, L3_gnn_msg_w, L3_gnn_msg_b, L3_gnn_upd_w, L3_gnn_upd_b, L3_gnn_ln_w, L3_gnn_ln_b):
    import jax
    import jax.numpy as jnp
    def _L0_gnn_ref(h, node_adj, edge_adj, W, a):
        import jax, jax.numpy as jnp
        import numpy as np
        N = 8192
        F_IN = 128
        F_OUT = 128
        ALPHA = 0.2
        NEG_INF = -9000000000000000.0

        def _signed_adj(key, n, p=0.002):
            r = jax.random.uniform(key, (n, n), dtype=jnp.float32)
            return jnp.where(r < p, 1.0, jnp.where(r > 1.0 - p, -1.0, 0.0)).astype(jnp.float32)
        hw = h @ W
        pos = (node_adj > 0).astype(hw.dtype)
        neg = (node_adj < 0).astype(hw.dtype)
        h_plus = pos @ hw
        h_minus = neg @ hw
        a1, a2 = (a[:F_OUT], a[F_OUT:])
        e_plus = jax.nn.leaky_relu((h_plus @ a1 + h_minus @ a2)[:, 0], ALPHA)
        e_minus = jax.nn.leaky_relu((h_minus @ a1 + h_plus @ a2)[:, 0], ALPHA)
        scores = jnp.where(edge_adj > 0, e_plus[None, :], NEG_INF)
        scores = jnp.where(edge_adj < 0, e_minus[None, :], scores)
        attn = jax.nn.softmax(scores, axis=1)
        h_prime = attn * edge_adj @ hw
        return h_prime

    def _L1_gnn_ref(H, A, W, b):
        import jax, jax.numpy as jnp
        import numpy as np
        N = 8192
        IN_DIM = 128
        OUT_DIM = 128
        EDGE_P = 0.002
        n = A.shape[0]
        A_t = A + jnp.eye(n, dtype=A.dtype)
        D = A_t.sum(axis=1)
        D_inv = jnp.where(D > 0, D ** (-0.5), jnp.zeros_like(D))
        A_norm = D_inv[:, None] * A_t * D_inv[None, :]
        HW = H @ W.T + b
        return jax.nn.relu(A_norm @ HW)

    def _L2_gnn_ref(x, adj, W, a):
        import jax, jax.numpy as jnp
        import numpy as np
        N, IN_DIM, OUT_DIM, HEADS = (4096, 128, 32, 4)
        EDGE_PROB = 0.015
        n = x.shape[0]
        xp = (x @ W).reshape(n, HEADS, OUT_DIM)
        a_j, a_i = (a[:OUT_DIM], a[OUT_DIM:])
        s_j = jnp.einsum('nhd,d->nh', xp, a_j)
        s_i = jnp.einsum('nhd,d->nh', xp, a_i)
        scale = jnp.float32(1.0 / np.sqrt(OUT_DIM))
        e = (s_i[:, None, :] + s_j[None, :, :]) * scale
        e = e + ((1.0 - adj) * jnp.float32(-1000000000.0))[:, :, None]
        att = jax.nn.softmax(e, axis=1)
        out = jnp.einsum('ijh,jhd->ihd', att, xp)
        return out.reshape(n, HEADS * OUT_DIM)

    def _L3_gnn_ref(node_feats, adj, msg_w, msg_b, upd_w, upd_b, ln_w, ln_b):
        import jax, jax.numpy as jnp
        import numpy as np
        LN_EPS = 1e-05
        D = node_feats.shape[-1]
        s = node_feats @ msg_w[:, :D].T
        d = node_feats @ msg_w[:, D:].T
        messages = jax.nn.gelu(s[:, None, :] + d[None, :, :] + msg_b, approximate=False)
        aggregated = jnp.einsum('ijd,ij->id', messages, adj)
        combined = jnp.concatenate([node_feats, aggregated], axis=-1)
        new_feats = combined @ upd_w.T + upd_b
        h = jax.nn.gelu(new_feats, approximate=False) + node_feats
        mu = jnp.mean(h, axis=-1, keepdims=True)
        var = jnp.var(h, axis=-1, keepdims=True)
        return (h - mu) / jnp.sqrt(var + LN_EPS) * ln_w + ln_b

    x = _layernorm(x + _L0_gnn_ref(x, adj, adj, L0_gnn_W, L0_gnn_a), axis=-1)
    x = _layernorm(x + _L1_gnn_ref(x, adj, L1_gnn_W, L1_gnn_b), axis=-1)
    x = _layernorm(x + _L2_gnn_ref(x, adj, L2_gnn_W, L2_gnn_a), axis=-1)
    x = _layernorm(x + _L3_gnn_ref(x, adj, L3_gnn_msg_w, L3_gnn_msg_b, L3_gnn_upd_w, L3_gnn_upd_b, L3_gnn_ln_w, L3_gnn_ln_b), axis=-1)
    return x


_drawn_inputs = setup_inputs


def setup_inputs(seed=0):
    import zlib

    import numpy as np

    out = dict(_drawn_inputs(seed))
    spreads = {'L3_gnn_ln_w': (1.0, 0.2), 'L3_gnn_ln_b': (0.0, 0.1)}
    factors = {'L3_gnn_upd_b': 3.414}
    for name, (base, spread) in spreads.items():
        noise = np.random.default_rng([zlib.crc32(name.encode()), seed]).standard_normal(out[name].shape)
        drawn = base * np.exp(spread * noise) if base else spread * noise
        out[name] = jnp.asarray(drawn.astype(out[name].dtype))
    for name, factor in factors.items():
        out[name] = (out[name] * factor).astype(out[name].dtype)
    return out
```

```python
from contextlib import ExitStack

import concourse.bass as bass
from concourse import mybir

F32 = mybir.dt.float32
BF16 = mybir.dt.bfloat16
I32 = mybir.dt.int32
U32 = mybir.dt.uint32
ALU = mybir.AluOpType
ACT = mybir.ActivationFunctionType
AX = mybir.AxisListType

P = 128
D = 128
HEADS, HD = 4, 32
PAIRS = 11
PAIR, SECOND = 246, 120
NB = 2 * PAIRS
OWN = (SECOND, PAIR - SECOND)
KM = 14
KX = 16
KO = 28
SEG = 170
NSEG = 16
WIDE = SEG * NSEG
NEG_INF = 9.0e15
SLOPE = 0.2
EPS = 1e-5
BANK = 512
W0, W2, W3 = D + 1, D + HEADS, D
O1, O2, O3 = 2 * D + 1, D + HEADS, 3 * D


def wait_apart(eng, always, waits):
    waits = [(s, v if isinstance(v, int) else eng.to_reg(v)) for s, v in waits if not (isinstance(v, int) and v == 0)]
    eng.wait_ge(always, 1)
    for s, v in waits:
        eng.wait_ge(s, v)


class Steps:

    def __init__(self, eng, sem, per_call=0, always=None):
        self.eng, self.sem, self.per_call, self.always = eng, sem, per_call, always
        self.base, self.count = 0, 0

    def call(self, n):
        assert self.count in (0, self.per_call), self.count
        self.base, self.count = n * self.per_call, 0

    def done(self, instruction, apart=False):
        instruction.then_inc(self.sem, 1)
        self.count += 1
        if apart:
            wait_apart(self.eng, self.always, [(self.sem, self.base + self.count)])
        else:
            self.eng.wait_ge(self.sem, self.base + self.count)


def build(nc, x, xT, adj, adjT, w0, w0T, a0, w1T, b1, w2, w2T, a2, wsT, wdT, msg_b, u1T, u2T, upd_b, ln_w, ln_b, out):
    N = x.shape[0]
    LAST = NB - 1
    assert N == PAIR * (PAIRS - 1) + SECOND + P and WIDE >= N

    def dram(name, shape):
        return nc.dram_tensor(name, shape, F32).ap()

    near0 = dram("near0", (N, W0))
    own1 = dram("own1", (N, O1))
    near2 = dram("near2", (N, W2))
    own2 = dram("own2", (N, O2))
    near3 = dram("near3", (N, W3))
    own3 = dram("own3", (N, O3))
    epem = [dram(f"e{c}", (N, 1)) for c in range(2)]
    sj = [dram(f"sj{c}", (N, 1)) for c in range(HEADS)]

    ctx = ExitStack()
    with ctx:
        def sb(name, shape, dt=F32):
            return ctx.enter_context(nc.sbuf_tensor(name, shape, dt))

        def sem(name):
            return ctx.enter_context(nc.semaphore(name))

        def flat(buffer, at, n, w):
            return buffer[:, :, :].rearrange("p a b -> p (a b)")[:, at:at + n * w].rearrange("p (n w) -> p n w", w=w)

        ident = sb("ident", [P, P])
        ones = sb("ones", [P, P])
        before = sb("before", [P, P])
        counting = sb("counting", [P, P])
        row_id = sb("row_id", [P, NB])
        owned = sb("owned", [P, NB])
        w0_s, w0T_s, w1T_s = sb("w0_s", [P, D]), sb("w0T_s", [P, D]), sb("w1T_s", [P, D])
        w2c = sb("w2c", [P, D + 2 * HEADS])
        w2T_s = sb("w2T_s", [P, D])
        a2_s = sb("a2_s", [P, 2 * HEADS])
        w3c = sb("w3c", [P, 3 * D])
        u2T_s = sb("u2T_s", [P, D])
        a0_s = sb("a0_s", [P, 1])
        wa = sb("wa", [P, P])
        b1_b, b3_b = sb("b1_b", [P, D]), sb("b3_b", [P, 2 * D])
        lnw_b, lnb_b = sb("lnw_b", [P, D]), sb("lnb_b", [P, D])
        eps = sb("eps", [P, 1])
        wa_sum = sb("wa_sum", [P, 1])
        thr = sb("thr", [P, 1])

        xT_s = sb("xT_s", [P, N])
        u1_b = sb("u1_b", [P, N])
        junk = sb("junk", [P, NB * P])
        rows = sb("rows", [P, 4, WIDE])
        cols = sb("cols", [P, 2, N])
        G = sb("G", [P, KO, W2])
        prod = sb("prod", [P, KO, D])
        xt4 = sb("xt4", [P, 4, P])
        hw4 = sb("hw4", [P, 4, W0])
        z4 = sb("z4", [P, 4])
        wa1 = sb("wa1", [P, 1])
        neg = sb("neg", [P, NB])
        junkb = sb("junkb", [P, N], BF16)
        zero = sb("zero", [1, P + BANK])
        cand = sb("cand", [P, NSEG * 8])
        cand2 = sb("cand2", [P, NSEG * 8])
        top = sb("top", [P, KX])
        ix = sb("ix", [P, 2, KX], U32)
        Vall = sb("Vall", [P, NB, KX])
        Iall = sb("Iall", [P, NB, KX], U32)
        Vo = sb("Vo", [P, KO + 4])
        Io = sb("Io", [P, KO + 4], U32)
        flags = sb("flags", [P, 4])
        bad = sb("bad", [P, 4])
        bads = sb("bads", [P, 1])
        flag = sb("flag", [P, 1], I32)
        zz, ez, ee = sb("zz", [P, 4]), sb("ez", [P, 2]), sb("ee", [P, 2])
        dpos = sb("dpos", [P, 1])
        over = sb("over", [P, NB])
        okay = sb("okay", [P, NB])
        psn = sb("psn", [P, 3, NB])
        found = sb("found", [P, 2])
        gid = sb("gid", [P, 1], I32)
        sid = sb("sid", [P, 1], I32)
        sidf = sb("sidf", [P, 1])
        xo = sb("xo", [P, 3, D])
        sc = sb("sc", [P, 3, KO, HEADS])
        pr = sb("pr", [P, KO, HEADS])
        wgt = sb("wgt", [P, KO])
        Z = sb("Z", [P, HEADS])
        rz = sb("rz", [P, HEADS])
        nmx = sb("nmx", [P, HEADS])
        dsum = sb("dsum", [P, 1])
        t = sb("t", [P, D])
        t2 = sb("t2", [P, D])
        st6 = sb("st6", [P, 6])
        mv = sb("mv", [P, 2])
        std = sb("std", [P, 2])
        rstd = sb("rstd", [P, 1])
        xTb = sb("xTb", [P, P])
        hwm = sb("hwm", [P, 2, D])
        o1 = sb("o1", [P, 2, O1])
        own1_all = flat(rows, 0, NB, O1)
        GP = PAIRS
        st6g = sb("st6g", [P, GP, 6])
        mvg = sb("mvg", [P, NB, 2])
        stdg = sb("stdg", [P, NB])
        rstdg = sb("rstdg", [P, NB])
        tg = sb("tg", [P, GP, D])
        x2T = sb("x2T", [P, GP, D])
        n2t = flat(rows, NB * O1, NB, W2)
        o2t = flat(cols, 0, NB, O2)
        in2 = sb("in2", [P, 2, O2])
        in3 = sb("in3", [P, 2, O3])
        in2s = sb("in2s", [P, O2])
        in3s = sb("in3s", [P, O3])
        rid2 = sb("rid2", [P, NB, 2])
        n3t = sb("n3t", [P, 2, W3])
        o3 = sb("o3", [P, 2, O3])
        yt = sb("yt", [P, 2, D])
        ps = ctx.enter_context(nc.psum_tensor("ps", [P, 8 * BANK], F32))
        acc = ps[:, 6 * BANK:6 * BANK + D]
        trn = ps[:, 6 * BANK + D:6 * BANK + 2 * D]
        threes = [(q, min(3, GP - q)) for q in range(0, GP, 3)]

        def hw_ps(r):
            return ps[:, (6 + r % 2) * BANK:(6 + r % 2) * BANK + D]

        def yps(g):
            return ps[:, 3 * g * BANK:3 * g * BANK + GP * D].rearrange("p (q d) -> p q d", d=D)

        def p2ps(c, m):
            at, w = (6 + c % 2) * BANK, D + 2 * HEADS
            return ps[:, at:at + m * w].rearrange("p (q w) -> p q w", w=w)

        prj = ps[:, 7 * BANK:8 * BANK]

        def two(name):
            return [sem(name + "_a"), sem(name + "_b")]

        s_iota, s_const, s_zero = sem("s_iota"), sem("s_const"), sem("s_zero")
        s_w, s_w2, s_x = sem("s_w"), sem("s_w2"), sem("s_x")
        s_wa, s_wac, s_u, s_uc = sem("s_wa"), sem("s_wac"), sem("s_u"), sem("s_uc")
        s_w2a, s_w2ac, s_was = sem("s_w2a"), sem("s_w2ac"), sem("s_was")
        q_row = [sem(f"q_row{r}") for r in range(4)]
        q_xt = [sem(f"q_xt{r}") for r in range(4)]
        q_z = [sem(f"q_z{r}") for r in range(4)]
        q_neg = [sem(f"q_neg{r}") for r in range(4)]
        q_e = [sem(f"q_e{r}") for r in range(4)]
        q_hw = [sem(f"q_hw{r}") for r in range(4)]
        q_hwc = [sem(f"q_hwc{r}") for r in range(4)]
        q_st = [sem(f"q_st{r}") for r in range(4)]
        s_row, s_col, s_xo, s_ix, s_st1 = two("s_row"), two("s_col"), two("s_xo"), two("s_ix"), two("s_st1")
        s_g, s_prod, s_acc, s_x1, s_hwm, s_y, s_o1 = (two("s_g"), two("s_prod"), two("s_acc"), two("s_x1"), two("s_hwm"),
                                                      two("s_y"), two("s_o1"))
        s_ex, s_c0 = sem("s_ex"), sem("s_c0")
        s_sc, s_p, s_mv, s_std, s_trn, s_xTb, s_prj = (sem("s_sc"), sem("s_p"), sem("s_mv"), sem("s_std"), sem("s_trn"),
                                                       sem("s_xTb"), sem("s_prj"))
        s_ov, s_pos, s_ovp, s_oh, s_list, s_ids = sem("s_ov"), sem("s_pos"), sem("s_ovp"), sem("s_oh"), sem("s_list"), sem("s_ids")
        s_orow, s_ocol, s_oxo, s_oex, s_scat1 = (sem("s_orow"), sem("s_ocol"), sem("s_oxo"), sem("s_oex"),
                                                        sem("s_scat1"))
        s_yc, s_o1a, s_o1n, s_yT, s_c1, s_mvg, s_sg = (sem("s_yc"), sem("s_o1a"), sem("s_o1n"), sem("s_yT"), sem("s_c1"),
                                                       sem("s_mvg"), sem("s_sg"))
        s_x2, s_x2T, s_x2c, s_p2, s_p2c, s_st2 = sem("s_x2"), sem("s_x2T"), sem("s_x2c"), sem("s_p2"), sem("s_p2c"), sem("s_st2")
        f_sum, f_gelu = two("f_sum"), two("f_gelu")
        s_c2, s_c3, f_nf, f_h = sem("s_c2"), sem("s_c3"), sem("f_nf"), sem("f_h")

        s_bad, s_flag, s_fdone = sem("s_bad"), sem("s_flag"), sem("s_fdone")
        g_w, g_wa, g_wac, g_u, g_uc = sem("g_w"), sem("g_wa"), sem("g_wac"), sem("g_u"), sem("g_uc")
        g_in = {l: sem(f"g_in_{l}") for l in (1, 0, 2, 3)}
        g_dve = {l: sem(f"g_dve_{l}") for l in (1, 0, 2, 3)}
        g_act = {l: sem(f"g_act_{l}") for l in (0, 2, 3)}
        g_pe = {l: sem(f"g_pe_{l}") for l in (0, 2, 3)}
        g_st = {l: sem(f"g_st_{l}") for l in (1, 0, 2, 3)}
        g_rows = {l: sem(f"g_rows_{l}") for l in (0, 2, 3)}
        g_prod = {l: sem(f"g_prod_{l}") for l in (0, 2, 3)}
        g_acc = {l: sem(f"g_acc_{l}") for l in (0, 2, 3)}
        g_sj, g_sum, g_gelu, g_last = sem("g_sj"), sem("g_sum"), sem("g_gelu"), sem("g_last")

        block = ctx.enter_context(nc.Block())
        OVER = (NB, PAIRS, 0)

        def apart(eng, *waits):
            wait_apart(eng, s_const, waits)

        def past(l, h):
            return l * (PAIRS + 1 - h)

        def past_gathers(l, h):
            return 16 * l * (KM * PAIRS + (KO if h == 0 else 0))

        def rows_of(it, h):
            return it * PAIR + h * SECOND

        def own(n, h):
            return P if isinstance(n, int) and n == NB - 1 else OWN[h]

        def all_but_last(eng, body):
            for h in range(2):
                body(h, 0, h, True)
            with eng.Fori(1, PAIRS - 1) as it:
                for h in range(2):
                    body(it * 2 + h, it, h, True)

        def free(eng, semaphore, value):
            if not (isinstance(value, int) and value == 0):
                eng.wait_ge(semaphore, value)

        def pairs(eng, body):
            all_but_last(eng, body)
            for h in range(2):
                body(NB - 2 + h, PAIRS - 1, h, False)

        def quads(eng, body):
            for r in range(4):
                body(r, 0, r, rows_of(r // 2, r % 2))
            with eng.Fori(1, NB // 4) as it:
                for r in range(4):
                    body(it * 4 + r, it, r, it * (2 * PAIR) + rows_of(r // 2, r % 2))
            for r in range(NB % 4):
                body(NB - 2 + r, NB // 4, r, rows_of(PAIRS - 1, r))

        def gathered(h):
            return G[:, h * KM:(h + 1) * KM, :]

        chunks = [(c, min(BANK, N - c)) for c in range(0, N, BANK)]

        def mm(pe, dst, lhsT, rhs, start, stop):
            return pe.matmul(dst, lhsT, rhs, start=start, stop=stop, skip_group_check=True)

        def layer1_io(sp, r):
            for h in range(2):
                sp.dma_start(own1_all[:, h::2, :],
                             bass.AP(own1.tensor, rows_of(0, h) * O1, [[O1, P], [PAIR * O1, PAIRS], [1, O1]])).then_inc(s_o1a, 16)
            sp.wait_ge(s_p2c, 8 * r + 8)
            for t_, table, w in ((n2t, near2, W2), (o2t, own2, O2)):
                for h in range(2):
                    sp.dma_start(bass.AP(table.tensor, rows_of(0, h) * w, [[w, OWN[h]], [PAIR * w, PAIRS], [1, w]]),
                                 t_[0:OWN[h], h::2, :]).then_inc(s_st2, 16)
                sp.dma_start(table[N - P + OWN[1]:N, :], t_[OWN[1]:P, NB - 1, :]).then_inc(s_st2, 16)
            sp.wait_ge(s_st2, 16 * 6 * (r + 1))

        def layer1_act(act, r):
            for at, m in chunks:
                act.activation(xT_s[:, at:at + m], ps[:, at:at + m], ACT.Copy).then_inc(s_yc, 1)
            for g in range(2):
                act.wait_ge(s_mvg, 2 * r + g + 1)
                act.activation(stdg[:, g * GP:(g + 1) * GP], mvg[:, g * GP:(g + 1) * GP, 1], ACT.Sqrt,
                               bias=eps[:, 0:1]).then_inc(s_sg, 1)
                act.wait_ge(s_x2T, 2 * r + g + 1)
                if g:
                    act.wait_ge(s_p2, 8 * r + 4 * g)
                act.activation(x2T[:, :, :], yps(g), ACT.Copy).then_inc(s_x2c, 1)
                for c, (q, m) in enumerate(threes):
                    act.wait_ge(s_p2, 8 * r + 4 * g + c + 1)
                    src = p2ps(c, m)
                    n = g * GP + q
                    act.activation(n2t[:, n:n + m, :], src[:, :, 0:W2], ACT.Copy)
                    act.activation(o2t[:, n:n + m, D:O2], src[:, :, W2:W2 + HEADS], ACT.Copy).then_inc(s_p2c, 1)

        def layer1_pe(pe, r):
            pe.wait_ge(s_yc, len(chunks) * (r + 1))
            for g in range(2):
                for q in range(GP):
                    n = g * GP + q
                    start = rows_of(n // 2, n % 2)
                    last = pe.transpose(yps(g)[:, q, :], xT_s[:, start:start + P], ident[:, :])
                last.then_inc(s_yT, 1)
            for g in range(2):
                pe.wait_ge(s_x2, 2 * r + g + 1)
                for q in range(GP):
                    last = pe.transpose(yps(g)[:, q, :], o2t[:, g * GP + q, 0:D], ident[:, :])
                last.then_inc(s_x2T, 1)
                pe.wait_ge(s_x2c, 2 * r + g + 1)
                for c, (q, m) in enumerate(threes):
                    if 8 * r + 4 * g + c >= 2:
                        pe.wait_ge(s_p2c, 8 * r + 4 * g + c - 1)
                    for k in range(m):
                        last = mm(pe, p2ps(c, m)[:, k, :], x2T[:, q + k, :], w2c[:, :], True, True)
                    last.then_inc(s_p2, 1)

        def layer1_dve(dve, r):
            c1 = Steps(dve, s_c1)
            c1.base = r * 10
            for g in range(2):
                at = slice(g * GP, (g + 1) * GP)
                dve.wait_ge(s_yT, 2 * r + g + 1)
                dve.wait_ge(s_o1a, 32 * (r + 1))
                if g:
                    dve.wait_ge(s_x2, 2 * r + g)
                c1.done(dve.tensor_tensor(tg[:, :, :], yps(g), own1_all[:, at, D:2 * D], ALU.add))
                c1.done(dve.tensor_tensor(tg[:, :, :], tg[:, :, :], own1_all[:, at, 2 * D:O1].broadcast_to([P, GP, D]), ALU.mult))
                c1.done(dve.scalar_tensor_tensor(out=tg[:, :, :], in0=tg[:, :, :], scalar=0.0, in1=own1_all[:, at, 0:D],
                                                 op0=ALU.max, op1=ALU.add))
                for q in range(GP):
                    last = dve.bn_stats(st6g[:, q, :], tg[:, q, :])
                c1.done(last)
                for q in range(GP):
                    last = dve.bn_aggr(mvg[:, g * GP + q, :], st6g[:, q, :])
                last.then_inc(s_mvg, 1)
                dve.wait_ge(s_sg, 2 * r + g + 1)
                c1.done(dve.reciprocal(rstdg[:, at], stdg[:, at]))
                for q in range(GP):
                    n = g * GP + q
                    last = dve.tensor_scalar(o2t[:, n, 0:D], tg[:, q, :], mvg[:, n, 0:1], rstdg[:, n:n + 1], ALU.subtract,
                                             ALU.mult)
                last.then_inc(s_x2, 1)

            assert c1.count == 10

        TURNS = -(-N // KO)
        TAIL = N - KO * (TURNS - 1)

        def general_if_needed(eng, path):
            eng.wait_ge(s_flag, 1)
            with eng.If(eng.value_load(flag[0:1, 0:1], min_val=0, max_val=1) > 0):
                path(eng)

        def every_block(eng, body):
            with eng.Fori(0, PAIRS) as it:
                for h in range(2):
                    body(it * 2 + h, it, h)

        def every_turn(eng, n, body):
            with eng.Fori(0, TURNS - 1) as c:
                body(n * TURNS + c, c * KO, KO)
            body(n * TURNS + (TURNS - 1), (TURNS - 1) * KO, TAIL)

        DVE0 = dict(scores=10, weights=12, stats=15, normal=19, hw=22)
        DVE2 = dict(mask=2, stats=19, normal=21, table=23)
        DVE3 = dict(nf=1, stats=4, stats2=11, out=13)
        ACT0, ACT2, ACT3 = dict(p=1, std=2, xTb=3), dict(p=HEADS, std=HEADS + 1, xTb=HEADS + 2), dict(aT=1, h=2, std=3, std2=4)
        PE0, PE2, PE3 = dict(trn=1, prj=2, y=3), dict(trn=1, prj=2), dict(prj=1)

        def step(n, steps, name):
            return n * max(steps.values()) + steps[name]

        def head_step(n, hd, k):
            return n * DVE2["table"] + (DVE2["mask"] + 3 * hd + k)

        def general_sp(sp):
            sp.dma_start(a0_s[:, :], a0[D:2 * D, :]).then_inc(g_w, 16)
            sp.dma_start(xT_s[:, :], xT).then_inc(g_w, 16)

            def own_rows(n, it, h, table, src):
                return table[bass.ds(rows_of(it, h), OWN[h]), :], src[0:OWN[h], :]

            def last_two(table, src):
                sp.dma_start(table[N - P + OWN[1]:N, :], src[OWN[1]:P, :]).then_inc(g_last, 16)

            def first(n, it, h):
                sp.dma_start(rows[:, 0, 0:N], adj[bass.ds(rows_of(it, h), P), :]).then_inc(g_in[1], 16)
                apart(sp, (g_dve[1], n * 3 + 3))
                sp.dma_start(*own_rows(n, it, h, epem[0], ee[:, 0:1])).then_inc(g_st[1], 16)
                sp.dma_start(*own_rows(n, it, h, epem[1], ee[:, 1:2])).then_inc(g_st[1], 16)
            every_block(sp, first)
            sp.wait_ge(g_st[1], 32 * NB)
            for c in range(2):
                last_two(epem[c], ee[:, c:c + 1])
            sp.wait_ge(g_last, 32)
            sp.dma_start(u1_b[:, :], epem[0].rearrange("n a -> (n a)").partition_broadcast(P)).then_inc(g_w, 16)
            sp.dma_start(cols[:, 1, :], epem[1].rearrange("n a -> (n a)").partition_broadcast(P)).then_inc(g_w, 16)

            def turns(n, l, table, w):
                def one(m, at, K):
                    sp.dma_start(G[:, 0:K, 0:w], table[bass.ds(at, K), :].partition_broadcast(P)).then_inc(g_rows[l], 16)
                    apart(sp, (g_prod[l], m + 1))
                every_turn(sp, n, one)

            def layer0(n, it, h):
                start = rows_of(it, h)
                sp.dma_start(rows[:, 0, 0:N], adj[bass.ds(start, P), :]).then_inc(g_in[0], 16)
                sp.dma_start(cols[:, 0, :], adjT[bass.ds(start, P), :]).then_inc(g_in[0], 16)
                sp.dma_start(xo[:, 0, :], x[bass.ds(start, P), :]).then_inc(g_in[0], 16)
                turns(n, 0, near0, W0)
                apart(sp, (g_dve[0], step(n, DVE0, "hw")))
                sp.dma_start(*own_rows(n, it, h, own1, o1[:, 0, :])).then_inc(g_st[0], 16)
                apart(sp, (g_pe[0], step(n, PE0, "y")))
            every_block(sp, layer0)
            last_two(own1, o1[:, 0, :])
            sp.wait_ge(g_st[0], 16 * NB)
            sp.wait_ge(g_last, 48)
            layer1_io(sp, 1)
            for c in range(HEADS):
                for h in range(2):
                    sp.dma_start(bass.AP(sj[c].tensor, rows_of(0, h), [[1, OWN[h]], [PAIR, PAIRS], [1, 1]]),
                                 n2t[0:OWN[h], h::2, D + c:D + c + 1], allow_slow_non_contiguous=True).then_inc(g_st[2], 16)
                sp.dma_start(sj[c][N - P + OWN[1]:N, :], n2t[OWN[1]:P, NB - 1, D + c:D + c + 1]).then_inc(g_st[2], 16)
            sp.wait_ge(g_st[2], 16 * 3 * HEADS)

            def layer2(n, it, h):
                start = rows_of(it, h)
                sp.dma_start(cols[:, 0, :], adj[bass.ds(start, P), :]).then_inc(g_in[2], 16)
                sp.dma_start(in2[:, 0, :], own2[bass.ds(start, P), :]).then_inc(g_in[2], 16)
                for c in range(HEADS):
                    sp.dma_start(u1_b[:, :], sj[c].rearrange("n a -> (n a)").partition_broadcast(P)).then_inc(g_sj, 16)
                    apart(sp, (g_dve[2], head_step(n, c, 1)))
                turns(n, 2, near2, W2)
                apart(sp, (g_dve[2], step(n, DVE2, "table")))
                sp.dma_start(*own_rows(n, it, h, near3, n3t[:, 0, :])).then_inc(g_st[2], 16)
                sp.dma_start(*own_rows(n, it, h, own3, o3[:, 0, :])).then_inc(g_st[2], 16)
            every_block(sp, layer2)
            last_two(near3, n3t[:, 0, :])
            last_two(own3, o3[:, 0, :])
            sp.wait_ge(g_st[2], 16 * 3 * HEADS + 32 * NB)
            sp.wait_ge(g_last, 80)

            def layer3(n, it, h):
                start = rows_of(it, h)
                sp.dma_start(rows[:, 0, 0:N], adj[bass.ds(start, P), :]).then_inc(g_in[3], 16)
                sp.dma_start(in3[:, 0, :], own3[bass.ds(start, P), :]).then_inc(g_in[3], 16)
                turns(n, 3, near3, W3)
                apart(sp, (g_dve[3], step(n, DVE3, "out")))
                sp.dma_start(*own_rows(n, it, h, out, yt[:, 0, :])).then_inc(g_st[3], 16)
            every_block(sp, layer3)
            last_two(out, yt[:, 0, :])
            sp.wait_ge(g_st[3], 16 * NB)
            sp.wait_ge(g_last, 96)

        def general_act(act):
            for c, (at, m) in enumerate(chunks):
                act.wait_ge(g_u, c + 1)
                act.activation(cols[:, 1, at:at + m], ps[:, at:at + m], ACT.Copy).then_inc(g_uc, 1)

            def layer0(n, it, h):
                act.wait_ge(g_dve[0], step(n, DVE0, "scores"))
                act.activation(rows[:, 1, 0:N], rows[:, 1, 0:N], ACT.Exp, bias=nmx[:, 0:1], accum_out=Z[:, 0:1]).then_inc(g_act[0], 1)
                act.wait_ge(g_dve[0], step(n, DVE0, "stats"))
                act.activation(std[:, 1:2], dsum[:, :], ACT.Sqrt)
                act.activation(std[:, 0:1], mv[:, 1:2], ACT.Sqrt, bias=eps[:, 0:1]).then_inc(g_act[0], 1)
                act.wait_ge(g_pe[0], step(n, PE0, "trn"))
                act.activation(xTb[:, :], trn, ACT.Copy).then_inc(g_act[0], 1)
            every_block(act, layer0)
            act.wait_ge(g_pe[0], NB * PE0["y"])
            layer1_act(act, 1)

            def layer2(n, it, h):
                for c in range(HEADS):
                    act.wait_ge(g_dve[2], head_step(n, c, 3))
                    act.activation(rows[:, c, 0:N], rows[:, c, 0:N], ACT.Exp, bias=nmx[:, c:c + 1],
                                   accum_out=Z[:, c:c + 1]).then_inc(g_act[2], 1)
                act.wait_ge(g_dve[2], step(n, DVE2, "stats"))
                act.activation(std[:, 0:1], mv[:, 1:2], ACT.Sqrt, bias=eps[:, 0:1]).then_inc(g_act[2], 1)
                act.wait_ge(g_pe[2], step(n, PE2, "trn"))
                act.activation(xTb[:, :], trn, ACT.Copy).then_inc(g_act[2], 1)
            every_block(act, layer2)

            def layer3(n, it, h):
                def gelu(m, at, K):
                    act.wait_ge(g_sum, m + 1)
                    act.activation(prod[:, 0:K, :], prod[:, 0:K, :], ACT.Gelu).then_inc(g_gelu, 1)
                every_turn(act, n, gelu)
                act.wait_ge(g_acc[3], n * TURNS + TURNS)
                act.activation(xTb[:, :], acc, ACT.Copy).then_inc(g_act[3], 1)
                act.wait_ge(g_dve[3], step(n, DVE3, "nf"))
                act.activation(t2[:, :], t[:, :], ACT.Gelu).then_inc(g_act[3], 1)
                for name in ("stats", "stats2"):
                    act.wait_ge(g_dve[3], step(n, DVE3, name))
                    act.activation(std[:, 0:1], mv[:, 1:2], ACT.Sqrt, bias=eps[:, 0:1]).then_inc(g_act[3], 1)
            every_block(act, layer3)

        def general_pe(pe):
            pe.wait_ge(g_w, 32)
            mm(pe, ps[:, 0:1], w0T_s[:, :], a0_s[:, :], True, True).then_inc(g_wa, 1)
            pe.wait_ge(g_wac, 1)
            for at, m in chunks:
                mm(pe, ps[:, at:at + m], wa[:, :], xT_s[:, at:at + m], True, True).then_inc(g_u, 1)
            pe.wait_ge(g_uc, len(chunks))
            for at, m in chunks:
                mm(pe, ps[:, at:at + m], zero[0:1, 0:P], zero[0:1, P:P + m], True, False)

            def sums(n, l, transposed):
                mm(pe, acc, zero[0:1, 0:P], zero[0:1, P:P + D], True, False)

                def one(m, at, K):
                    pe.wait_ge(g_prod[l], m + 1)
                    for k in range(K):
                        a, b = (prod[:, k, :], ident[:, :]) if transposed else (ident[:, :], prod[:, k, :])
                        last = mm(pe, acc, a, b, False, K == TAIL and k == K - 1)
                    last.then_inc(g_acc[l], 1)
                every_turn(pe, n, one)

            def layer0(n, it, h):
                pe.wait_ge(g_dve[0], step(n, DVE0, "weights"))
                sums(n, 0, False)
                pe.wait_ge(g_dve[0], step(n, DVE0, "normal"))
                pe.transpose(trn, o1[:, 0, 0:D], ident[:, :]).then_inc(g_pe[0], 1)
                pe.wait_ge(g_act[0], step(n, ACT0, "xTb"))
                mm(pe, prj[:, 0:D], xTb[:, :], w1T_s[:, :], True, True).then_inc(g_pe[0], 1)
                pe.wait_ge(g_dve[0], step(n, DVE0, "hw"))
                for at, m in chunks:
                    last = mm(pe, ps[:, at:at + m], hwm[:, 0, :], cols[:, 0, at:at + m], False, False)
                last.then_inc(g_pe[0], 1)
            every_block(pe, layer0)
            layer1_pe(pe, 1)

            def layer2(n, it, h):
                pe.wait_ge(g_dve[2], head_step(n, HEADS - 1, 3))
                sums(n, 2, False)
                pe.wait_ge(g_dve[2], step(n, DVE2, "normal"))
                pe.transpose(trn, o3[:, 0, 0:D], ident[:, :]).then_inc(g_pe[2], 1)
                pe.wait_ge(g_act[2], step(n, ACT2, "xTb"))
                mm(pe, prj[:, 0:3 * D], xTb[:, :], w3c[:, :], True, True).then_inc(g_pe[2], 1)
            every_block(pe, layer2)

            def layer3(n, it, h):
                pe.wait_ge(g_in[3], n * 32 + 32)
                sums(n, 3, True)
                pe.wait_ge(g_act[3], step(n, ACT3, "aT"))
                mm(pe, prj[:, 0:D], xTb[:, :], u2T_s[:, :], True, True).then_inc(g_pe[3], 1)
            every_block(pe, layer3)

        def general_dve(dve):
            dve.wait_ge(g_wa, 1)
            g = Steps(dve, g_wac)
            dve.tensor_copy(wa1[:, :], ps[:, 0:1]).then_inc(s_was, 1)
            dve.wait_ge(s_was, 2)
            dve.tensor_scalar(wa[:, :], ones[:, :], wa1[:, 0:1], None, ALU.mult).then_inc(g_wac, 1)
            dve.wait_ge(g_uc, len(chunks))

            e = Steps(dve, g_dve[1], 3, s_const)

            def first(n, it, h):
                e.call(n)
                dve.wait_ge(g_in[1], n * 16 + 16)
                a = rows[:, 0, 0:N]
                for k, (sign, u) in enumerate([(ALU.is_gt, u1_b[:, :]), (ALU.is_lt, cols[:, 1, :]),
                                               (ALU.is_lt, u1_b[:, :]), (ALU.is_gt, cols[:, 1, :])]):
                    last = dve.scalar_tensor_tensor(out=rows[:, k % 2 + 1, 0:N] if k < 2 else rows[:, 3, 0:N] if k == 2 else junk[:, 0:N],
                                                    in0=a, scalar=0.0, in1=u, op0=sign,
                                                    op1=ALU.mult, accum_out=zz[:, k:k + 1])
                e.done(last)
                e.done(dve.tensor_reduce(ez[:, :], zz[:, :].rearrange("p (s k) -> p s k", k=2), AX.X, ALU.add))
                e.done(dve.scalar_tensor_tensor(out=ee[:, :], in0=ez[:, :], scalar=SLOPE, in1=ez[:, :], op0=ALU.mult,
                                                op1=ALU.max))
                dve.wait_ge(g_st[1], n * 32 + 32)
            every_block(dve, first)
            dve.wait_ge(g_w, 64)

            def turns(n, l, product):
                def one(m, at, K):
                    dve.wait_ge(g_rows[l], m * 16 + 16)
                    product(m, at, K).then_inc(g_prod[l], 1)
                    dve.wait_ge(g_acc[l], m + 1)
                every_turn(dve, n, one)

            def stats(steps, src):
                steps.done(dve.bn_stats(st6[:, :], src), True)
                steps.done(dve.bn_aggr(mv[:, :], st6[:, :]))

            d0 = Steps(dve, g_dve[0], DVE0["hw"], s_const)

            def layer0(n, it, h):
                d0.call(n)
                dve.wait_ge(g_in[0], n * 48 + 48)
                a, s, w = rows[:, 0, 0:N], rows[:, 1, 0:N], rows[:, 3, 0:N]
                d0.done(dve.tensor_reduce(dsum[:, :], a, AX.X, ALU.add))
                d0.done(dve.tensor_scalar(st6[:, 0:1], dsum[:, :], 1.0, None, ALU.add))
                d0.done(dve.tensor_scalar(dpos[:, :], st6[:, 0:1], 0.0, None, ALU.is_gt))
                d0.done(dve.tensor_scalar(dsum[:, :], st6[:, 0:1], 1e-34, None, ALU.max))
                d0.done(dve.scalar_tensor_tensor(out=s, in0=a, scalar=0.0, in1=u1_b[:, :], op0=ALU.is_gt, op1=ALU.mult))
                d0.done(dve.scalar_tensor_tensor(out=w, in0=a, scalar=0.0, in1=cols[:, 1, :], op0=ALU.is_lt, op1=ALU.mult))
                d0.done(dve.tensor_tensor(s, s, w, ALU.add))
                d0.done(dve.tensor_scalar(w, a, 0.0, -NEG_INF, ALU.is_equal, ALU.mult))
                d0.done(dve.tensor_tensor(s, s, w, ALU.add))
                d0.done(dve.tensor_reduce(nmx[:, 0:1], s, AX.X, ALU.max, negate=True))
                dve.wait_ge(g_act[0], step(n, ACT0, "p"))
                d0.done(dve.tensor_tensor(w, s, a, ALU.mult))
                d0.done(dve.reciprocal(rz[:, 0:1], Z[:, 0:1]), True)
                turns(n, 0, lambda m, at, K: dve.tensor_tensor(
                    prod[:, 0:K, :], G[:, 0:K, 0:D], rows[:, 3, bass.ds(at, K)].unsqueeze(2).broadcast_to([P, K, D]), ALU.mult))
                d0.done(dve.scalar_tensor_tensor(out=t[:, :], in0=acc, scalar=rz[:, 0:1], in1=xo[:, 0, :], op0=ALU.mult,
                                                 op1=ALU.add))
                stats(d0, t[:, :])
                dve.wait_ge(g_act[0], step(n, ACT0, "std"))
                d0.done(dve.reciprocal(st6[:, 0:1], std[:, 1:2]))
                d0.done(dve.tensor_tensor(o1[:, 0, 2 * D:O1], st6[:, 0:1], dpos[:, :], ALU.mult))
                d0.done(dve.reciprocal(rstd[:, :], std[:, 0:1]))
                d0.done(dve.tensor_scalar(o1[:, 0, 0:D], t[:, :], mv[:, 0:1], rstd[:, 0:1], ALU.subtract, ALU.mult))
                dve.wait_ge(g_pe[0], step(n, PE0, "prj"))
                d0.done(dve.tensor_tensor(t[:, :], prj[:, 0:D], b1_b[:, :], ALU.add))
                d0.done(dve.tensor_scalar(o1[:, 0, D:2 * D], t[:, :], o1[:, 0, 2 * D:O1], None, ALU.mult))
                d0.done(dve.tensor_scalar(hwm[:, 0, :], o1[:, 0, D:2 * D], owned[:, bass.ds(n, 1)], None, ALU.mult))
                dve.wait_ge(g_st[0], n * 16 + 16)
                dve.wait_ge(g_pe[0], step(n, PE0, "y"))
            every_block(dve, layer0)
            layer1_dve(dve, 1)
            dve.wait_ge(g_st[2], 16 * 3 * HEADS)

            d2 = Steps(dve, g_dve[2], DVE2["table"], s_const)

            def layer2(n, it, h):
                d2.call(n)
                dve.wait_ge(g_in[2], n * 32 + 32)
                a, pen = cols[:, 0, :], cols[:, 1, :]
                d2.done(dve.tensor_scalar(a, a, -1.0, 1.0, ALU.mult, ALU.add))
                d2.done(dve.tensor_scalar(pen, a, -1.0e9, None, ALU.mult))
                for c in range(HEADS):
                    dve.wait_ge(g_sj, n * (16 * HEADS) + 16 * (c + 1))
                    d2.done(dve.tensor_scalar(rows[:, c, 0:N], u1_b[:, :], in2[:, 0, D + c:D + c + 1], None, ALU.add))
                    d2.done(dve.scalar_tensor_tensor(out=rows[:, c, 0:N], in0=rows[:, c, 0:N], scalar=HD ** -0.5, in1=pen,
                                                     op0=ALU.mult, op1=ALU.add))
                    d2.done(dve.tensor_reduce(nmx[:, c:c + 1], rows[:, c, 0:N], AX.X, ALU.max, negate=True))
                dve.wait_ge(g_act[2], step(n, ACT2, "p"))
                d2.done(dve.reciprocal(rz[:, :], Z[:, :]), True)
                turns(n, 2, lambda m, at, K: dve.tensor_tensor(
                    prod[:, 0:K, :].rearrange("p k (c d) -> p k c d", c=HEADS),
                    G[:, 0:K, 0:D].rearrange("p k (c d) -> p k c d", c=HEADS),
                    rows[:, :, bass.ds(at, K)].rearrange("p c k -> p k c").unsqueeze(3).broadcast_to([P, K, HEADS, HD]), ALU.mult))
                d2.done(dve.tensor_tensor(t[:, :].rearrange("p (c d) -> p c d", c=HEADS), acc.rearrange("p (c d) -> p c d", c=HEADS),
                                          rz[:, :].unsqueeze(2).broadcast_to([P, HEADS, HD]), ALU.mult))
                d2.done(dve.tensor_tensor(t2[:, :], t[:, :], in2[:, 0, 0:D], ALU.add))
                stats(d2, t2[:, :])
                dve.wait_ge(g_act[2], step(n, ACT2, "std"))
                d2.done(dve.reciprocal(rstd[:, :], std[:, 0:1]))
                d2.done(dve.tensor_scalar(o3[:, 0, 0:D], t2[:, :], mv[:, 0:1], rstd[:, 0:1], ALU.subtract, ALU.mult))
                dve.wait_ge(g_pe[2], step(n, PE2, "prj"))
                d2.done(dve.tensor_copy(n3t[:, 0, :], prj[:, 0:D]))
                d2.done(dve.tensor_tensor(o3[:, 0, D:O3], prj[:, D:O3], b3_b[:, :], ALU.add))
                dve.wait_ge(g_st[2], n * 32 + (16 * 3 * HEADS + 32))
            every_block(dve, layer2)

            d3 = Steps(dve, g_dve[3], DVE3["out"], s_const)

            def layer3(n, it, h):
                d3.call(n)
                apart(dve, (g_in[3], n * 32 + 32))
                mine = in3[:, 0, :]

                def message(m, at, K):
                    dve.tensor_tensor(prod[:, 0:K, :], G[:, 0:K, 0:D], mine[:, D:2 * D].unsqueeze(1).broadcast_to([P, K, D]),
                                      ALU.add).then_inc(g_sum, 1)
                    dve.wait_ge(g_gelu, m + 1)
                    return dve.tensor_tensor(prod[:, 0:K, :], prod[:, 0:K, :],
                                             rows[:, 0, bass.ds(at, K)].unsqueeze(2).broadcast_to([P, K, D]), ALU.mult)
                turns(n, 3, message)
                dve.wait_ge(g_pe[3], step(n, PE3, "prj"))
                d3.done(dve.tensor_tensor(t[:, :], prj[:, 0:D], mine[:, 2 * D:3 * D], ALU.add))
                dve.wait_ge(g_act[3], step(n, ACT3, "h"))
                d3.done(dve.tensor_tensor(t[:, :], t2[:, :], mine[:, 0:D], ALU.add))
                stats(d3, t[:, :])
                dve.wait_ge(g_act[3], step(n, ACT3, "std"))
                d3.done(dve.reciprocal(rstd[:, :], std[:, 0:1]))
                d3.done(dve.tensor_scalar(t[:, :], t[:, :], mv[:, 0:1], rstd[:, 0:1], ALU.subtract, ALU.mult))
                d3.done(dve.tensor_tensor(t[:, :], t[:, :], lnw_b[:, :], ALU.mult))
                d3.done(dve.tensor_tensor(t[:, :], t[:, :], lnb_b[:, :], ALU.add))
                d3.done(dve.tensor_tensor(t[:, :], t[:, :], mine[:, 0:D], ALU.add))
                stats(d3, t[:, :])
                dve.wait_ge(g_act[3], step(n, ACT3, "std2"))
                d3.done(dve.reciprocal(rstd[:, :], std[:, 0:1]))
                d3.done(dve.tensor_scalar(yt[:, 0, :], t[:, :], mv[:, 0:1], rstd[:, 0:1], ALU.subtract, ALU.mult))
                dve.wait_ge(g_st[3], n * 16 + 16)
            every_block(dve, layer3)

        @block.sync
        def _(sp):
            sp.dma_start(w0T_s[:, :], w0T).then_inc(s_w, 16)
            sp.dma_start(a0_s[:, :], a0[0:D, :]).then_inc(s_w, 16)
            sp.dma_start(xT_s[:, :], xT).then_inc(s_x, 16)
            sp.dma_start(w0_s[:, :], w0).then_inc(s_w, 16)

            def first_pass(n, it, r, start):
                apart(sp, (q_z[r], it))
                free(sp, q_neg[r], it)
                sp.dma_start(rows[:, r, 0:N], adj[bass.ds(start, P), :]).then_inc(q_row[r], 16)
                apart(sp, (q_hw[r], it))
                sp.dma_start(xt4[:, r, :], xT[:, bass.ds(start, P)]).then_inc(q_xt[r], 16)
            quads(sp, first_pass)

            sp.wait_ge(s_const, 1)
            for dst, src in [(w1T_s[:, :], w1T), (w2c[:, 0:D], w2), (w2T_s[:, :], w2T), (w3c[:, 0:D], wdT),
                             (w3c[:, D:2 * D], wsT), (w3c[:, 2 * D:3 * D], u1T), (u2T_s[:, :], u2T),
                             (b1_b[:, :], b1.partition_broadcast(P)), (b3_b[:, 0:D], msg_b.partition_broadcast(P)),
                             (b3_b[:, D:2 * D], upd_b.partition_broadcast(P)),
                             (lnw_b[:, :], ln_w.partition_broadcast(P)), (lnb_b[:, :], ln_b.partition_broadcast(P))]:
                sp.dma_start(dst, src).then_inc(s_w2, 16)
            for c in range(2):
                for g in range(HEADS):
                    sp.dma_start(a2_s[HD * g:HD * g + HD, HEADS * c + g:HEADS * c + g + 1],
                                 a2[HD * c:HD * c + HD].rearrange("(d a) -> d a", a=1)).then_inc(s_w2, 16)

            for h in range(2):
                sp.wait_ge(q_z[h], NB // 4 + 1)
                sp.wait_ge(q_neg[h], NB // 4 + 1)
                sp.dma_start(rows[:, h, 0:N], adj[rows_of(0, h):rows_of(0, h) + P, :]).then_inc(s_row[h], 16)

            def layer0(n, it, h, more):
                start = rows_of(it, h)
                if more:
                    apart(sp, (s_ix[h], it + 1))
                    sp.dma_start(rows[:, h, 0:N], adj[bass.ds(start + PAIR, P), :]).then_inc(s_row[h], 16)
                apart(sp, (s_x1[h], it))
                sp.dma_start(xo[:, h, :], x[bass.ds(start, P), :]).then_inc(s_xo[h], 16)
                apart(sp, (s_y[h], it))
                sp.dma_start(cols[:, h, :], adjT[bass.ds(start, P), :]).then_inc(s_col[h], 16)
            pairs(sp, layer0)

            sp.wait_ge(s_scat1, 16)
            layer1_io(sp, 0)

            def layer2(n, it, h, more):
                apart(sp, (s_x1[h], it + past(1, h)))
                sp.dma_start(in2[:, h, :], own2[bass.ds(rows_of(it, h), P), :]).then_inc(s_xo[h], 16)
            pairs(sp, layer2)

            sp.wait_ge(s_scat1, 16 * 3)

            def layer3(n, it, h, more):
                apart(sp, (s_o1[h], it + past(1, h)))
                sp.dma_start(in3[:, h, :], own3[bass.ds(rows_of(it, h), P), :]).then_inc(s_xo[h], 16)
            pairs(sp, layer3)
            sp.wait_ge(s_scat1, 16 * 4)
            for h in range(2):
                sp.wait_ge(s_st1[h], 64 * PAIRS)
            general_if_needed(sp, general_sp)

        @block.gpsimd
        def _(pool):
            pool.memset(ident[:, :], 0.0).then_inc(s_iota, 1)
            pool.memset(before[:, :], 1.0).then_inc(s_iota, 1)
            pool.iota(counting[:, :], pattern=[[1, P]], base=1, channel_multiplier=0,
                      allow_small_or_imprecise_dtypes=True).then_inc(s_iota, 1)
            pool.iota(row_id[:, :], pattern=[[PAIR, PAIRS], [SECOND, 2]], base=0, channel_multiplier=1,
                      allow_small_or_imprecise_dtypes=True).then_inc(s_iota, 1)
            pool.memset(owned[:, :], 1.0).then_inc(s_iota, 1)
            pool.memset(rows[:, :, N:WIDE], 0.0).then_inc(s_iota, 1)
            pool.wait_ge(s_iota, 6)
            pool.affine_select(out=ident[:, :], in_=ident[:, :], compare_op=ALU.not_equal, fill=1.0, base=0,
                               pattern=[[-1, P]], channel_multiplier=1).then_inc(s_iota, 1)
            pool.affine_select(out=before[:, :], in_=before[:, :], compare_op=ALU.is_gt, fill=0.0, base=0,
                               pattern=[[1, P]], channel_multiplier=-1).then_inc(s_iota, 1)
            for h, blocks in ((0, owned[:, 0:NB:2]), (1, owned[:, 1:NB - 1:2])):
                pool.affine_select(out=blocks, in_=blocks, compare_op=ALU.is_gt, fill=0.0, base=OWN[h],
                                   pattern=[[0, PAIRS - h]], channel_multiplier=-1).then_inc(s_iota, 1)

            def gather(dst, table, index, signal):
                pool.indirect_dma_start(out=dst, out_offset=None, in_=table,
                                        in_offset=bass.IndirectOffsetOnAxis(ap=index, axis=0),
                                        bounds_check=N - 1, oob_is_err=False).then_inc(signal, 16)

            def scatter(table, src, signal):
                pool.indirect_dma_start(out=table, out_offset=bass.IndirectOffsetOnAxis(ap=sid[:, 0:1], axis=0), in_=src,
                                        in_offset=None, bounds_check=N - 1, oob_is_err=False).then_inc(signal, 16)

            def main_gathers(l, free, free_past, table, width):
                def one(n, it, h, more):
                    apart(pool, (s_ix[h], it + 1 + l * PAIRS))
                    apart(pool, (free[h], it + free_past(h)))
                    for k in range(KM):
                        gather(G[:, h * KM + k, 0:width], table[:, :], ix[:, h, k:k + 1], s_g[h])
                return one

            def over_gathers(free, free_past, table, width):
                for h in range(2):
                    pool.wait_ge(free[h], PAIRS + free_past(h))
                for k in range(KO):
                    gather(G[:, k, 0:width], table[:, :], Io[:, k:k + 1], s_g[0])

            for r in range(4):
                pool.wait_ge(q_st[r], 16 * (6 if r < 2 else 5))
            stage = main_gathers(0, s_prod, lambda h: 0, near0, W0)
            all_but_last(pool, stage)
            stage(NB - 2, PAIRS - 1, 0, False)
            pool.wait_ge(s_ids, 2)
            gather(rows[:, 2, 0:N], adj[:, :], gid[:, 0:1], s_orow)
            gather(rows[:, 3, 0:N], adjT[:, :], gid[:, 0:1], s_ocol)
            gather(xo[:, 2, :], x[:, :], gid[:, 0:1], s_oxo)
            stage(NB - 1, PAIRS - 1, 1, False)
            pool.wait_ge(s_oex, 11)
            over_gathers(s_prod, lambda h: 0, near0, W0)
            for h in range(2):
                pool.wait_ge(s_st1[h], 16 * PAIRS)
            pool.wait_ge(s_hwm[0], PAIRS + 1)
            scatter(own1[:, :], o1[:, 0, :], s_scat1)

            pool.wait_ge(s_st2, 16 * 6)
            gather(in2s[:, :], own2[:, :], gid[:, 0:1], s_oxo)
            pairs(pool, main_gathers(1, s_prod, lambda h: past(1, h), near2, W2))
            over_gathers(s_prod, lambda h: past(1, h), near2, W2)
            for h in range(2):
                pool.wait_ge(s_st1[h], 48 * PAIRS)
            pool.wait_ge(s_o1[0], PAIRS + 1 + past(0, 0))
            scatter(near3[:, :], n3t[:, 0, :], s_scat1)
            scatter(own3[:, :], o3[:, 0, :], s_scat1)
            pool.wait_ge(s_scat1, 16 * 3)
            gather(in3s[:, :], own3[:, :], gid[:, 0:1], s_oxo)
            pairs(pool, main_gathers(2, f_sum, lambda h: 0, near3, W3))
            over_gathers(f_sum, lambda h: 0, near3, W3)
            for h in range(2):
                pool.wait_ge(s_st1[h], 64 * PAIRS)
            pool.wait_ge(s_o1[0], PAIRS + 1 + past(1, 0))
            scatter(out[:, :], yt[:, 0, :], s_scat1)
            pool.wait_ge(s_scat1, 16 * 4)

        @block.scalar
        def _(act):
            act.wait_ge(s_zero, 1)
            for c, (at, m) in enumerate(chunks):
                act.wait_ge(s_u, c + 1)
                act.activation(u1_b[:, at:at + m], ps[:, at:at + m], ACT.Copy).then_inc(s_uc, 1)

            def first_pass(n, it, r, start):
                act.wait_ge(q_row[r], it * 16 + 16)
                act.activation(junkb[:, :], rows[:, r, 0:N], ACT.Relu, scale=-1.0,
                               accum_out=neg[:, bass.ds(n, 1)]).then_inc(q_neg[r], 1)
                free(act, q_st[r], it * 16)
                act.wait_ge(q_hw[r], it + 1)
                act.activation(hw4[:, r, 0:D], hw_ps(r), ACT.Copy).then_inc(q_hwc[r], 1)
                act.wait_ge(q_hwc[r], it + 1)
                act.wait_ge(q_e[r], it + 1)
                m = own(n, r % 2)
                act.dma_start(near0[bass.ds(start, m), :], hw4[0:m, r, :]).then_inc(q_st[r], 16)
            quads(act, first_pass)

            def layer0(n, it, h, K):
                act.wait_ge(s_sc, n + 1)
                act.activation(pr[:, 0:K, 0], sc[:, 0, 0:K, 0], ACT.Exp, bias=nmx[:, 0:1], accum_out=Z[:, 0:1]).then_inc(s_p, 1)
                act.wait_ge(s_mv, n + 1)
                act.activation(std[:, 1:2], dsum[:, :], ACT.Sqrt, bias=ones[:, 0:1])
                act.activation(std[:, 0:1], mv[:, 1:2], ACT.Sqrt, bias=eps[:, 0:1]).then_inc(s_std, 1)
                act.wait_ge(s_trn, n + 1)
                act.activation(xTb[:, :], trn, ACT.Copy).then_inc(s_xTb, 1)

            def layer0_main(n, it, h, more):
                layer0(n, it, h, KM)
                act.wait_ge(s_hwm[h], it + 1)
                m = own(n, h)
                act.dma_start(own1[bass.ds(rows_of(it, h), m), :], o1[0:m, h, :]).then_inc(s_st1[h], 16)
            pairs(act, layer0_main)
            layer0(*OVER, KO)

            act.wait_ge(s_y[0], PAIRS + 1)
            layer1_act(act, 0)

            def layer2(n, it, h, K):
                act.wait_ge(s_sc, n + 1 + 1 * (NB + 1))
                act.activation(pr[:, 0:K, :], sc[:, 2, 0:K, :], ACT.Exp).then_inc(s_p, 1)
                act.wait_ge(s_mv, n + 1 + 1 * (NB + 1))
                act.activation(std[:, 0:1], mv[:, 1:2], ACT.Sqrt, bias=eps[:, 0:1]).then_inc(s_std, 1)
                act.wait_ge(s_trn, n + 1 + 1 * (NB + 1))
                act.activation(xTb[:, :], trn, ACT.Copy).then_inc(s_xTb, 1)

            def layer2_main(n, it, h, more):
                layer2(n, it, h, KM)
                act.wait_ge(s_o1[h], it + 1 + past(0, h))
                m = own(n, h)
                start = rows_of(it, h)
                act.dma_start(near3[bass.ds(start, m), :], n3t[0:m, h, :]).then_inc(s_st1[h], 16)
                act.dma_start(own3[bass.ds(start, m), :], o3[0:m, h, :]).then_inc(s_st1[h], 16)
            pairs(act, layer2_main)
            layer2(*OVER, KO)

            def layer3(n, it, h, K):
                act.wait_ge(f_sum[h], it + 1)
                part = prod[:, h * KM:h * KM + K, :]
                act.activation(part, part, ACT.Gelu).then_inc(f_gelu[h], 1)
                act.wait_ge(s_acc[h], it + 1 + past(2, h))
                act.activation(xTb[:, :], acc, ACT.Copy).then_inc(s_xTb, 1)
                act.wait_ge(f_nf, n + 1)
                act.activation(t2[:, :], t[:, :], ACT.Gelu).then_inc(f_h, 1)
                for k in range(2):
                    act.wait_ge(s_mv, n * 2 + (k + 1) + 2 * (NB + 1))
                    act.activation(std[:, 0:1], mv[:, 1:2], ACT.Sqrt, bias=eps[:, 0:1]).then_inc(s_std, 1)

            def layer3_main(n, it, h, more):
                layer3(n, it, h, KM)
                act.wait_ge(s_o1[h], it + 1 + past(1, h))
                m = own(n, h)
                act.dma_start(out[bass.ds(rows_of(it, h), m), :], yt[0:m, h, :]).then_inc(s_st1[h], 16)
            pairs(act, layer3_main)
            layer3(*OVER, KO)
            for h in range(2):
                act.wait_ge(s_st1[h], 64 * PAIRS)
            general_if_needed(act, general_act)

        @block.tensor
        def _(pe):
            pe.wait_ge(s_w, 16 * 3)
            mm(pe, ps[:, 0:1], w0T_s[:, :], a0_s[:, :], True, True).then_inc(s_wa, 1)
            pe.wait_ge(s_wac, 1)
            pe.wait_ge(s_x, 16)
            for at, m in chunks:
                mm(pe, ps[:, at:at + m], wa[:, :], xT_s[:, at:at + m], True, True).then_inc(s_u, 1)

            def first_pass(n, it, r, start):
                pe.wait_ge(q_xt[r], it * 16 + 16)
                free(pe, q_hwc[(r + 2) % 4], it + r // 2)
                mm(pe, hw_ps(r), xt4[:, r, :], w0_s[:, :], True, True).then_inc(q_hw[r], 1)
            quads(pe, first_pass)

            pe.wait_ge(s_w2, 16 * 20)
            pe.wait_ge(q_hwc[1], NB // 4 + 1)
            mm(pe, prj[:, 0:2 * HEADS], w2T_s[:, :], a2_s[:, :], True, True).then_inc(s_w2a, 1)
            pe.wait_ge(s_w2ac, 1)
            mm(pe, prj[:, 8:9], ones[:, :], wa_sum[:, :], True, True).then_inc(s_w2a, 1)
            pe.wait_ge(s_uc, len(chunks))
            pe.wait_ge(s_zero, 1)
            for at, m in chunks:
                mm(pe, ps[:, at:at + m], zero[0:1, 0:P], zero[0:1, P:P + m], True, False)

            def layer0(n, it, h, K, columns):
                pe.wait_ge(s_prod[h], it + 1)
                for k in range(K):
                    last = mm(pe, acc, ident[:, :], prod[:, h * KM + k, :], k == 0, k == K - 1)
                last.then_inc(s_acc[h], 1)
                pe.wait_ge(s_x1[h], it + 1)
                pe.transpose(trn, o1[:, h, 0:D], ident[:, :]).then_inc(s_trn, 1)
                pe.wait_ge(s_xTb, n + 1)
                mm(pe, prj[:, 0:D], xTb[:, :], w1T_s[:, :], True, True).then_inc(s_prj, 1)
                pe.wait_ge(s_hwm[h], it + 1)
                for at, m in chunks:
                    last = mm(pe, ps[:, at:at + m], hwm[:, h, :], columns[:, at:at + m], False, K == KO)
                last.then_inc(s_y[h], 1)

            def layer0_main(n, it, h, more):
                pe.wait_ge(s_col[h], it * 16 + 16)
                layer0(n, it, h, KM, cols[:, h, :])

            all_but_last(pe, layer0_main)
            pe.wait_ge(s_ov, 1)
            mm(pe, prj[:, 0:NB], before[:, :], over[:, :], True, True)
            mm(pe, prj[:, NB:2 * NB], ones[:, :], over[:, :], True, True).then_inc(s_ovp, 1)
            pe.wait_ge(s_oh, 1)
            for n in range(NB):
                last = mm(pe, prj[:, 2 * NB:2 * NB + 2], junk[:, n * P:(n + 1) * P], rid2[:, n, :], n == 0, n == NB - 1)
            last.then_inc(s_list, 1)
            for h in range(2):
                layer0_main(NB - 2 + h, PAIRS - 1, h, False)
            pe.wait_ge(s_ocol, 16)
            layer0(*OVER, KO, rows[:, 3, :])

            layer1_pe(pe, 0)

            def layer2(n, it, h, K):
                pe.wait_ge(s_prod[h], it + 1 + past(1, h))
                for k in range(K):
                    last = mm(pe, acc, ident[:, :], prod[:, h * KM + k, :], k == 0, k == K - 1)
                last.then_inc(s_acc[h], 1)
                pe.wait_ge(s_x1[h], it + 1 + past(1, h))
                pe.transpose(trn, o3[:, h, 0:D], ident[:, :]).then_inc(s_trn, 1)
                pe.wait_ge(s_xTb, n + 1 + 1 * (NB + 1))
                mm(pe, prj[:, 0:3 * D], xTb[:, :], w3c[:, :], True, True).then_inc(s_prj, 1)
            pairs(pe, lambda n, it, h, more: layer2(n, it, h, KM))
            layer2(*OVER, KO)

            def layer3(n, it, h, K):
                pe.wait_ge(s_prod[h], it + 1 + past(2, h))
                for k in range(K):
                    last = mm(pe, acc, prod[:, h * KM + k, :], ident[:, :], k == 0, k == K - 1)
                last.then_inc(s_acc[h], 1)
                pe.wait_ge(s_xTb, n + 1 + 2 * (NB + 1))
                mm(pe, prj[:, 0:D], xTb[:, :], u2T_s[:, :], True, True).then_inc(s_prj, 1)
            pairs(pe, lambda n, it, h, more: layer3(n, it, h, KM))
            layer3(*OVER, KO)
            pe.wait_ge(s_bad, 1)
            mm(pe, prj[:, 0:1], ones[:, :], bads[:, :], True, True).then_inc(s_bad, 1)
            general_if_needed(pe, general_pe)

        @block.vector
        def _(dve):
            dve.memset(a2_s[:, :], 0.0).then_inc(s_const, 1)
            dve.memset(ones[:, :], 1.0)
            dve.memset(zero[:, :], 0.0)
            dve.memset(eps[:, :], EPS).then_inc(s_zero, 1)
            dve.wait_ge(s_wa, 1)
            dve.wait_ge(s_zero, 1)
            dve.tensor_copy(wa1[:, :], ps[:, 0:1]).then_inc(s_was, 1)
            dve.wait_ge(s_was, 1)
            dve.tensor_scalar(wa[:, :], ones[:, :], wa1[:, 0:1], None, ALU.mult).then_inc(s_wac, 1)
            dve.wait_ge(s_uc, len(chunks))

            def first_pass(n, it, r, start):
                dve.wait_ge(q_row[r], it * 16 + 16)
                dve.scalar_tensor_tensor(out=junk[:, 0:N], in0=rows[:, r, 0:N], scalar=0.0, in1=u1_b[:, :], op0=ALU.is_gt,
                                         op1=ALU.mult, accum_out=z4[:, r:r + 1]).then_inc(q_z[r], 1)
                dve.wait_ge(q_z[r], it + 1)
                free(dve, q_st[r], it * 16)
                dve.scalar_tensor_tensor(out=hw4[:, r, D:W0], in0=z4[:, r:r + 1], scalar=SLOPE, in1=z4[:, r:r + 1],
                                         op0=ALU.mult, op1=ALU.max).then_inc(q_e[r], 1)
            quads(dve, first_pass)

            dve.wait_ge(s_w2a, 1)
            dve.tensor_copy(w2c[:, D:D + 2 * HEADS], prj[:, 0:2 * HEADS])
            dve.tensor_reduce(wa_sum[:, :], prj[:, 0:2 * HEADS], AX.X, ALU.add, apply_absolute_value=True).then_inc(s_w2ac, 1)
            dve.wait_ge(s_w2a, 2)
            dve.tensor_scalar(thr[:, :], prj[:, 8:9], 24 * HD ** -0.5 * 1e-9, 5e-7, ALU.mult, ALU.add)

            ex = Steps(dve, s_ex, 7, s_const)

            def segments(n, it, h):
                ex.call(n)
                apart(dve, (s_row[h], it * 16 + 16))
                for s in range(NSEG):
                    last = dve.max(cand[:, 8 * s:8 * s + 8], rows[:, h, SEG * s:SEG * (s + 1)])
                ex.done(last, True)

            def largest(n, it, h):
                ex.done(dve.max(top[:, 0:8], cand[:, :]), True)
                ex.done(dve.match_replace(cand2[:, :], top[:, 0:8], cand[:, :], 0.0), True)
                ex.done(dve.max(top[:, 8:16], cand2[:, :]), True)
                apart(dve, (s_g[h], it * (16 * KM)))
                dve.max_index(ix[:, h, 0:8], top[:, 0:8], rows[:, h, :])

            def seconds(n, it, h):
                last = dve.max_index(ix[:, h, 8:16], top[:, 8:16], rows[:, h, :])
                last.then_inc(s_ix[h], 1)

            def overflow_flags(n, it, h):
                dve.wait_ge(s_ix[h], it + 1)
                dve.tensor_copy(Iall[:, bass.ds(n, 1), :].rearrange("p a k -> p (a k)"), ix[:, h, :])
                dve.tensor_copy(Vall[:, bass.ds(n, 1), :].rearrange("p a k -> p (a k)"), top[:, :])
                dve.scalar_tensor_tensor(out=flags[:, 0:1], in0=top[:, 7:8], scalar=top[:, 8:9], in1=top[:, 7:8],
                                         op0=ALU.is_equal, op1=ALU.mult)
                dve.tensor_copy(flags[:, 1:2], top[:, KM:KM + 1])
                ex.done(dve.tensor_reduce(flags[:, 2:3], cand[:, 7::8], AX.X, ALU.max))
                ex.done(dve.tensor_reduce(flags[:, 3:4], flags[:, 0:3], AX.X, ALU.max))
                dve.scalar_tensor_tensor(out=over[:, bass.ds(n, 1)], in0=flags[:, 3:4], scalar=0.0,
                                         in1=owned[:, bass.ds(n, 1)], op0=ALU.is_gt, op1=ALU.mult)
                ex.done(dve.scalar_tensor_tensor(out=okay[:, bass.ds(n, 1)], in0=flags[:, 3:4], scalar=0.0,
                                                 in1=owned[:, bass.ds(n, 1)], op0=ALU.is_le, op1=ALU.mult))

            def extract(n, it, h):
                segments(n, it, h)
                largest(n, it, h)
                seconds(n, it, h)
                overflow_flags(n, it, h)

            def norm_stats(steps, src):
                steps.done(dve.bn_stats(st6[:, :], src), True)
                dve.bn_aggr(mv[:, :], st6[:, :]).then_inc(s_mv, 1)

            c0 = Steps(dve, s_c0, 9, s_const)

            def entries(n, K):
                return Vo[:, 0:K] if K == KO else Vall[:, bass.ds(n, 1), 0:K].rearrange("p a k -> p (a k)")

            def scores0(n, it, h, K):
                c0.call(n)
                V = entries(n, K)
                if K == KM:
                    dve.wait_ge(s_g[h], (it + 1) * (16 * KM))
                else:
                    dve.wait_ge(s_g[h], it * (16 * KM) + 16 * KO)
                dve.tensor_reduce(dsum[:, :], V, AX.X, ALU.add)
                c0.done(dve.tensor_scalar(sc[:, 1, 0:K, 0], V, 0.0, None, ALU.is_gt))
                dve.tensor_scalar(sc[:, 2, 0:K, 0], sc[:, 1, 0:K, 0], 1.0, NEG_INF, ALU.subtract, ALU.mult)
                c0.done(dve.tensor_tensor(sc[:, 1, 0:K, 1], G[:, h * KM:h * KM + K, D], sc[:, 1, 0:K, 0], ALU.mult))
                c0.done(dve.tensor_tensor(sc[:, 0, 0:K, 0], sc[:, 1, 0:K, 1], sc[:, 2, 0:K, 0], ALU.add))
                dve.tensor_reduce(nmx[:, 0:1], sc[:, 0, 0:K, 0], AX.X, ALU.max, negate=True).then_inc(s_sc, 1)

            def products0(n, it, h, K):
                dve.wait_ge(s_p, n + 1)
                dve.reciprocal(rz[:, 0:1], Z[:, 0:1])
                c0.done(dve.tensor_tensor(wgt[:, 0:K], pr[:, 0:K, 0], entries(n, K), ALU.mult))
                free(dve, s_acc[h], it)
                dve.tensor_tensor(prod[:, h * KM:h * KM + K, :], G[:, h * KM:h * KM + K, 0:D],
                                  wgt[:, 0:K].unsqueeze(2).broadcast_to([P, K, D]), ALU.mult).then_inc(s_prod[h], 1)

            def residual0(n, it, h, K):
                dve.wait_ge(s_acc[h], it + 1)
                if K == KM:
                    dve.wait_ge(s_xo[h], it * 16 + 16)
                else:
                    dve.wait_ge(s_oxo, 16)
                mine = xo[:, h if K == KM else 2, :]
                c0.done(dve.scalar_tensor_tensor(out=t[:, :], in0=acc, scalar=rz[:, 0:1], in1=mine, op0=ALU.mult, op1=ALU.add))
                norm_stats(c0, t[:, :])

            def normal0(n, it, h, K):
                dve.wait_ge(s_std, n + 1)
                dve.wait_ge(s_mv, n + 1)
                free(dve, s_st1[h], it * 16)
                dve.reciprocal(o1[:, h, 2 * D:O1], std[:, 1:2])
                c0.done(dve.reciprocal(rstd[:, :], std[:, 0:1]))
                dve.tensor_scalar(o1[:, h, 0:D], t[:, :], mv[:, 0:1], rstd[:, 0:1], ALU.subtract, ALU.mult).then_inc(s_x1[h], 1)

            def project0(n, it, h, K):
                dve.wait_ge(s_prj, n + 1)
                c0.done(dve.tensor_tensor(t[:, :], prj[:, 0:D], b1_b[:, :], ALU.add))
                c0.done(dve.tensor_scalar(o1[:, h, D:2 * D], t[:, :], o1[:, h, 2 * D:O1], None, ALU.mult))
                free(dve, s_y[h], it)
                ok = okay[:, bass.ds(n, 1)] if K == KM else found[:, 1:2]
                dve.tensor_scalar(hwm[:, h, :], o1[:, h, D:2 * D], ok, None, ALU.mult).then_inc(s_hwm[h], 1)

            dve.wait_ge(s_iota, 10)
            dve.wait_ge(s_w2, 16 * 20)
            for h in range(2):
                extract(h, 0, h)

            def layer0(n, it, h, more):
                scores0(n, it, h, KM)
                if more:
                    segments(n + 2, it + 1, h)
                products0(n, it, h, KM)
                if more:
                    largest(n + 2, it + 1, h)
                residual0(n, it, h, KM)
                if more:
                    seconds(n + 2, it + 1, h)
                normal0(n, it, h, KM)
                if more:
                    overflow_flags(n + 2, it + 1, h)
                project0(n, it, h, KM)

            all_but_last(dve, layer0)

            dve.tensor_copy(rid2[:, :, 0], row_id[:, :])
            dve.memset(rid2[:, :, 1], 1.0).then_inc(s_ov, 1)
            dve.wait_ge(s_ovp, 1)
            pos = Steps(dve, s_pos)
            pos.done(dve.tensor_copy(psn[:, 0, :], prj[:, NB:2 * NB]))
            pos.done(dve.tensor_tensor_scan(psn[:, 1, :], ones[:, 0:NB], psn[:, 0, :], 0.0, ALU.mult, ALU.add))
            pos.done(dve.tensor_tensor(psn[:, 0, :], psn[:, 1, :], psn[:, 0, :], ALU.subtract))
            pos.done(dve.tensor_tensor(psn[:, 2, :], prj[:, 0:NB], psn[:, 0, :], ALU.add))
            pos.done(dve.scalar_tensor_tensor(out=psn[:, 2, :], in0=psn[:, 2, :], scalar=1.0, in1=over[:, :], op0=ALU.add,
                                              op1=ALU.mult))
            dve.tensor_tensor(junk[:, :].rearrange("p (n c) -> p n c", c=P),
                              psn[:, 2, :].unsqueeze(2).broadcast_to([P, NB, P]),
                              counting[:, :].unsqueeze(1).broadcast_to([P, NB, P]), ALU.is_equal).then_inc(s_oh, 1)
            dve.wait_ge(s_list, 1)
            pos.done(dve.tensor_copy(found[:, :], prj[:, 2 * NB:2 * NB + 2]))
            dve.tensor_copy(gid[:, :], found[:, 0:1]).then_inc(s_ids, 1)
            pos.done(dve.tensor_scalar(sidf[:, :], found[:, 1:2], -2.0 * N, 2.0 * N, ALU.mult, ALU.add))
            dve.tensor_tensor(sid[:, :], sidf[:, :], found[:, 0:1], ALU.add).then_inc(s_ids, 1)

            layer0(NB - 2, PAIRS - 1, 0, False)
            oex = Steps(dve, s_oex)
            dve.wait_ge(s_orow, 16)
            for k in range((KO + 4) // 8):
                at = slice(8 * k, 8 * k + 8)
                oex.done(dve.max(Vo[:, at], rows[:, 2, :]))
                oex.done(dve.max_index(Io[:, at], Vo[:, at], rows[:, 2, :]))
                if k < (KO + 4) // 8 - 1:
                    oex.done(dve.match_replace(rows[:, 2, :], Vo[:, at], rows[:, 2, :], 0.0))
            layer0(NB - 1, PAIRS - 1, 1, False)
            for stage in (scores0, products0, residual0, normal0, project0):
                if stage is products0:
                    dve.wait_ge(s_acc[1], PAIRS)
                stage(*OVER, KO)
            c0.call(0)

            layer1_dve(dve, 0)

            def copy_indices(n, h):
                dve.tensor_copy(ix[:, h, :], Iall[:, bass.ds(n, 1), :].rearrange("p a k -> p (a k)")).then_inc(s_ix[h], 1)

            c2 = Steps(dve, s_c2, 11, s_const)

            def layer2(n, it, h, K, more):
                c2.call(n)
                V = entries(n, K)
                g = G[:, h * KM:h * KM + K, :]
                mine = in2[:, h, :] if K == KM else in2s[:, :]
                if K == KM:
                    dve.wait_ge(s_g[h], (it + 1) * (16 * KM) + past_gathers(1, h))
                    dve.wait_ge(s_xo[h], it * 16 + 16 + 1 * (16 * PAIRS))
                else:
                    dve.wait_ge(s_g[h], it * (16 * KM) + 16 * KO + past_gathers(1, h))
                    dve.wait_ge(s_oxo, 32)
                if more:
                    copy_indices(n + 2, h)
                c2.done(dve.tensor_scalar(wgt[:, 0:K], V, -1.0, 1.0, ALU.mult, ALU.add))
                c2.done(dve.tensor_scalar(wgt[:, 0:K], wgt[:, 0:K], -1.0e9, None, ALU.mult))
                c2.done(dve.tensor_tensor(sc[:, 0, 0:K, :], g[:, :, D:W2],
                                          mine[:, D:O2].unsqueeze(1).broadcast_to([P, K, HEADS]), ALU.add))
                c2.done(dve.scalar_tensor_tensor(out=sc[:, 1, 0:K, :], in0=sc[:, 0, 0:K, :], scalar=HD ** -0.5,
                                                 in1=wgt[:, 0:K].unsqueeze(2).broadcast_to([P, K, HEADS]), op0=ALU.mult,
                                                 op1=ALU.add))
                c2.done(dve.tensor_reduce(nmx[:, :], sc[:, 1, 0:K, :].rearrange("p k c -> p c k"), AX.X, ALU.max))
                dve.tensor_tensor(sc[:, 2, 0:K, :], sc[:, 1, 0:K, :], nmx[:, :].unsqueeze(1).broadcast_to([P, K, HEADS]),
                                  ALU.subtract).then_inc(s_sc, 1)
                dve.wait_ge(s_p, n + 1 + 1 * (NB + 1))
                dve.wait_ge(s_acc[h], it + past(1, h))
                if K == KO:
                    dve.wait_ge(s_acc[1], PAIRS + past(1, 1))
                dve.tensor_tensor(prod[:, h * KM:h * KM + K, :].rearrange("p k (c d) -> p k c d", c=HEADS),
                                  g[:, :, 0:D].rearrange("p k (c d) -> p k c d", c=HEADS),
                                  pr[:, 0:K, :].unsqueeze(3).broadcast_to([P, K, HEADS, HD]), ALU.mult).then_inc(s_prod[h], 1)
                c2.done(dve.tensor_reduce(Z[:, :], pr[:, 0:K, :].rearrange("p k c -> p c k"), AX.X, ALU.add))
                c2.done(dve.reciprocal(rz[:, :], Z[:, :]))
                dve.wait_ge(s_acc[h], it + 1 + past(1, h))
                c2.done(dve.tensor_tensor(t[:, :].rearrange("p (c d) -> p c d", c=HEADS), acc.rearrange("p (c d) -> p c d", c=HEADS),
                                          rz[:, :].unsqueeze(2).broadcast_to([P, HEADS, HD]), ALU.mult))
                c2.done(dve.tensor_tensor(t2[:, :], t[:, :], mine[:, 0:D], ALU.add))
                norm_stats(c2, t2[:, :])
                dve.wait_ge(s_std, n + 1 + 1 * (NB + 1))
                dve.wait_ge(s_mv, n + 1 + 1 * (NB + 1))
                dve.wait_ge(s_st1[h], it * 32 + 16 * PAIRS)
                c2.done(dve.reciprocal(rstd[:, :], std[:, 0:1]))
                dve.tensor_scalar(o3[:, h, 0:D], t2[:, :], mv[:, 0:1], rstd[:, 0:1], ALU.subtract, ALU.mult).then_inc(s_x1[h], 1)
                dve.wait_ge(s_prj, n + 1 + 1 * (NB + 1))
                dve.tensor_copy(n3t[:, h, :], prj[:, 0:D])
                dve.tensor_tensor(o3[:, h, D:O3], prj[:, D:O3], b3_b[:, :], ALU.add).then_inc(s_o1[h], 1)

            for h in range(2):
                copy_indices(h, h)
            pairs(dve, lambda n, it, h, more: layer2(n, it, h, KM, more))
            layer2(*OVER, KO, False)
            c2.call(0)

            c3 = Steps(dve, s_c3, 9, s_const)

            def layer3(n, it, h, K, more):
                c3.call(n)
                V = entries(n, K)
                mine = in3[:, h, :] if K == KM else in3s[:, :]
                part = prod[:, h * KM:h * KM + K, :]
                if K == KM:
                    dve.wait_ge(s_g[h], (it + 1) * (16 * KM) + past_gathers(2, h))
                    dve.wait_ge(s_xo[h], it * 16 + 16 + 2 * (16 * PAIRS))
                else:
                    dve.wait_ge(s_g[h], it * (16 * KM) + 16 * KO + past_gathers(2, h))
                    dve.wait_ge(s_oxo, 48)
                    dve.wait_ge(s_acc[1], PAIRS + past(2, 1))
                if more:
                    copy_indices(n + 2, h)
                dve.wait_ge(s_acc[h], it + past(2, h))
                dve.tensor_tensor(part, G[:, h * KM:h * KM + K, 0:D],
                                  mine[:, D:2 * D].unsqueeze(1).broadcast_to([P, K, D]), ALU.add).then_inc(f_sum[h], 1)
                dve.wait_ge(f_gelu[h], it + 1)
                dve.tensor_tensor(part, part, V.unsqueeze(2).broadcast_to([P, K, D]), ALU.mult).then_inc(s_prod[h], 1)
                dve.wait_ge(s_prj, n + 1 + 2 * (NB + 1))
                dve.tensor_tensor(t[:, :], prj[:, 0:D], mine[:, 2 * D:3 * D], ALU.add).then_inc(f_nf, 1)
                dve.wait_ge(f_h, n + 1)
                c3.done(dve.tensor_tensor(t[:, :], t2[:, :], mine[:, 0:D], ALU.add))
                norm_stats(c3, t[:, :])
                dve.wait_ge(s_mv, n * 2 + 1 + 2 * (NB + 1))
                dve.wait_ge(s_std, n * 2 + 1 + 2 * (NB + 1))
                c3.done(dve.reciprocal(rstd[:, :], std[:, 0:1]))
                c3.done(dve.tensor_scalar(t[:, :], t[:, :], mv[:, 0:1], rstd[:, 0:1], ALU.subtract, ALU.mult))
                c3.done(dve.tensor_tensor(t[:, :], t[:, :], lnw_b[:, :], ALU.mult))
                c3.done(dve.tensor_tensor(t[:, :], t[:, :], lnb_b[:, :], ALU.add))
                c3.done(dve.tensor_tensor(t[:, :], t[:, :], mine[:, 0:D], ALU.add))
                norm_stats(c3, t[:, :])
                dve.wait_ge(s_mv, n * 2 + 2 + 2 * (NB + 1))
                dve.wait_ge(s_std, n * 2 + 2 + 2 * (NB + 1))
                dve.wait_ge(s_st1[h], it * 16 + 48 * PAIRS)
                c3.done(dve.reciprocal(rstd[:, :], std[:, 0:1]))
                dve.tensor_scalar(yt[:, h, :], t[:, :], mv[:, 0:1], rstd[:, 0:1], ALU.subtract, ALU.mult).then_inc(s_o1[h], 1)

            dve.wait_ge(s_g[0], past_gathers(2, 0))
            for h in range(2):
                copy_indices(h, h)
            pairs(dve, lambda n, it, h, more: layer3(n, it, h, KM, more))
            layer3(*OVER, KO, False)
            c3.call(0)

            f = Steps(dve, s_fdone)
            dve.wait_ge(q_neg[0], NB // 4 + 1)
            dve.wait_ge(q_neg[1], NB // 4 + 1)
            dve.wait_ge(q_neg[2], NB // 4)
            dve.wait_ge(q_neg[3], NB // 4)
            f.done(dve.tensor_reduce(st6[:, 0:1], neg[:, :], AX.X, ALU.add))
            f.done(dve.tensor_reduce(st6[:, 1:2], Vall[:, :, 0], AX.X, ALU.min))
            f.done(dve.tensor_scalar(bad[:, 0:1], st6[:, 0:1], 0.0, None, ALU.is_gt))
            f.done(dve.tensor_tensor(bad[:, 1:2], st6[:, 1:2], thr[:, :], ALU.is_le))
            f.done(dve.tensor_scalar(bad[:, 2:3], psn[:, 1, NB - 1:NB], float(P), None, ALU.is_gt))
            f.done(dve.tensor_scalar(bad[:, 3:4], Vo[:, KO - 1:KO], 0.0, None, ALU.is_gt))
            dve.tensor_reduce(bads[:, :], bad[:, :], AX.X, ALU.add).then_inc(s_bad, 1)
            dve.wait_ge(s_bad, 2)
            f.done(dve.tensor_scalar(st6[:, 2:3], prj[:, 0:1], 0.5, None, ALU.is_gt))
            dve.tensor_copy(flag[:, :], st6[:, 2:3]).then_inc(s_flag, 1)
            general_if_needed(dve, general_dve)


def kernel(**inputs):
    import numpy as _np
    import concourse.bacc as _bacc
    from concourse import mybir as _mybir
    from concourse.bass_utils import run_bass_kernel_spmd as _run

    a = {k: _np.asarray(v) for k, v in inputs.items()}
    D = a["x"].shape[1]
    laid = {
        "x": a["x"], "xT": a["x"].T, "adj": a["adj"], "adjT": a["adj"].T,
        "w0": a["L0_gnn_W"], "w0T": a["L0_gnn_W"].T, "a0": a["L0_gnn_a"],
        "w1T": a["L1_gnn_W"].T, "b1": a["L1_gnn_b"],
        "w2": a["L2_gnn_W"], "w2T": a["L2_gnn_W"].T, "a2": a["L2_gnn_a"],
        "wsT": a["L3_gnn_msg_w"][:, :D].T, "wdT": a["L3_gnn_msg_w"][:, D:].T, "msg_b": a["L3_gnn_msg_b"],
        "u1T": a["L3_gnn_upd_w"][:, :D].T, "u2T": a["L3_gnn_upd_w"][:, D:].T, "upd_b": a["L3_gnn_upd_b"],
        "ln_w": a["L3_gnn_ln_w"], "ln_b": a["L3_gnn_ln_b"],
    }
    nc = _bacc.Bacc("TRN2", target_bir_lowering=False, num_devices=1)
    arrays, args = {}, {}
    for name, value in laid.items():
        v = _np.ascontiguousarray(value)
        arrays[f"in_{name}_dram"] = v
        args[name] = nc.dram_tensor(f"in_{name}_dram", v.shape, _mybir.dt.from_np(v.dtype), kind="ExternalInput").ap()
    args["out"] = nc.dram_tensor("out_0_dram", a["x"].shape, _mybir.dt.float32, kind="ExternalOutput").ap()
    build(nc, **args)
    r = _run(nc, [arrays], core_ids=[0])
    return r.results[0]["out_0_dram"]
```

```python
from contextlib import ExitStack

import concourse.bass as bass
from concourse import mybir

F32 = mybir.dt.float32
BF16 = mybir.dt.bfloat16
I32 = mybir.dt.int32
U32 = mybir.dt.uint32
ALU = mybir.AluOpType
ACT = mybir.ActivationFunctionType
AX = mybir.AxisListType

P = 128
D = 128
HEADS, HD = 4, 32
PAIRS = 11
PAIR, SECOND = 246, 120
NB = 2 * PAIRS
OWN = (SECOND, PAIR - SECOND)
KM = 14
KX = 16
KO = 24
SEGS, OSEGS = 8, 16
WIDE = 2720
NEG_INF = 9.0e15
SLOPE = 0.2
EPS = 1e-5
BANK = 512
W0, W2, W3 = D + 1, D + HEADS, D
O1, O2, O3 = 2 * D + 1, D + HEADS, 3 * D


def wait_apart(eng, always, waits):
    waits = [(s, v if isinstance(v, int) else eng.to_reg(v)) for s, v in waits if not (isinstance(v, int) and v == 0)]
    eng.wait_ge(always, 1)
    for s, v in waits:
        eng.wait_ge(s, v)


class Steps:

    def __init__(self, eng, sem, per_call=0, always=None):
        self.eng, self.sem, self.per_call, self.always = eng, sem, per_call, always
        self.base, self.count = 0, 0

    def call(self, n):
        assert self.count in (0, self.per_call), self.count
        self.base, self.count = n * self.per_call, 0

    def done(self, instruction, apart=False):
        instruction.then_inc(self.sem, 1)
        self.count += 1
        if apart:
            wait_apart(self.eng, self.always, [(self.sem, self.base + self.count)])
        else:
            self.eng.wait_ge(self.sem, self.base + self.count)


def build(nc, x, xT, adj, adjT, w0, w0T, a0, w1T, b1, w2, w2T, a2, wsT, wdT, msg_b, u1T, u2T, upd_b, ln_w, ln_b, out):
    N = x.shape[0]
    assert N == PAIR * (PAIRS - 1) + SECOND + P and WIDE >= N and WIDE % SEGS == WIDE % OSEGS == 0

    def dram(name, shape):
        return nc.dram_tensor(name, shape, F32).ap()

    near0 = dram("near0", (N, W0))
    own1 = dram("own1", (N, O1))
    near2 = dram("near2", (N, W2))
    own2 = dram("own2", (N, O2))
    near3 = dram("near3", (N, W3))
    own3 = dram("own3", (N, O3))
    epem = [dram(f"e{c}", (N, 1)) for c in range(2)]
    sj = [dram(f"sj{c}", (N, 1)) for c in range(HEADS)]

    ctx = ExitStack()
    with ctx:
        def sb(name, shape, dt=F32):
            return ctx.enter_context(nc.sbuf_tensor(name, shape, dt))

        def sem(name):
            return ctx.enter_context(nc.semaphore(name))

        def flat(buffer, at, n, w):
            return buffer[:, :, :].rearrange("p a b -> p (a b)")[:, at:at + n * w].rearrange("p (n w) -> p n w", w=w)

        ident = sb("ident", [P, P])
        ones = sb("ones", [P, P])
        others = sb("others", [P, P])
        before = sb("before", [P, P])
        counting = sb("counting", [P, P])
        row_id = sb("row_id", [P, NB])
        owned = sb("owned", [P, NB])
        w0_s, w0T_s, w1T_s = sb("w0_s", [P, D]), sb("w0T_s", [P, D]), sb("w1T_s", [P, D])
        w2c = sb("w2c", [P, D + 2 * HEADS])
        w2T_s = sb("w2T_s", [P, D])
        a2_s = sb("a2_s", [P, 2 * HEADS])
        w3c = sb("w3c", [P, 3 * D])
        u2T_s = sb("u2T_s", [P, D])
        a0_s = sb("a0_s", [P, 1])
        wa = sb("wa", [P, P])
        b1_b, b3_b = sb("b1_b", [P, D]), sb("b3_b", [P, 2 * D])
        lnw_b, lnb_b = sb("lnw_b", [P, D]), sb("lnb_b", [P, D])
        eps = sb("eps", [P, 1])
        wa_sum = sb("wa_sum", [P, 1])
        thr = sb("thr", [P, 1])

        xT_s = sb("xT_s", [P, N])
        u1_b = sb("u1_b", [P, N])
        junk = sb("junk", [P, NB * P])
        rows = sb("rows", [P, 4, WIDE])
        cols = sb("cols", [P, 2, N])
        G = sb("G", [P, 2 * KM, W2])
        prod = sb("prod", [P, 2 * KM, D])
        xt4 = sb("xt4", [P, 4, P])
        hw4 = sb("hw4", [P, 4, W0])
        z4 = sb("z4", [P, 4])
        wa1 = sb("wa1", [P, 1])
        neg = sb("neg", [P, NB])
        junkb = sb("junkb", [P, N], BF16)
        zero = sb("zero", [1, P + BANK])
        cand = sb("cand", [P, OSEGS * 8])
        cand2 = sb("cand2", [P, SEGS * 8])
        top = sb("top", [P, KX])
        ix = sb("ix", [P, 2, KX], U32)
        Vall = sb("Vall", [P, NB, KM])
        Iall = sb("Iall", [P, NB, KX], U32)
        Vo = sb("Vo", [P, KO])
        Io = sb("Io", [P, KO], U32)
        flags = sb("flags", [P, 4])
        bad = sb("bad", [P, 4])
        bads = sb("bads", [P, 1])
        flag = sb("flag", [P, 1], I32)
        zz, ez, ee = sb("zz", [P, 4]), sb("ez", [P, 2]), sb("ee", [P, 2])
        dpos = sb("dpos", [P, 1])
        over = sb("over", [P, NB])
        okay = sb("okay", [P, NB])
        psn = sb("psn", [P, 3, NB])
        found = sb("found", [P, 3])
        gid = sb("gid", [P, 1], I32)
        sid = sb("sid", [P, 1], I32)
        sidf = sb("sidf", [P, 1])
        xo = sb("xo", [P, 3, D])
        sc = sb("sc", [P, 3, KO, HEADS])
        pr = sb("pr", [P, KO, HEADS])
        wgt = sb("wgt", [P, KO])
        Z = sb("Z", [P, HEADS])
        rz = sb("rz", [P, 2 * HEADS])
        nmx = sb("nmx", [P, HEADS])
        dsum = sb("dsum", [P, 1])
        t = sb("t", [P, D])
        t2 = sb("t2", [P, D])
        st6 = sb("st6", [P, 6])
        mv = sb("mv", [P, 2])
        std = sb("std", [P, 2])
        rstd = sb("rstd", [P, 1])
        rok = sb("rok", [P, 2])
        xTb = sb("xTb", [P, P])
        hwm = sb("hwm", [P, 2, D])
        o1 = sb("o1", [P, 2, O1])
        own1_all = flat(rows, 0, NB, O1)
        GP = PAIRS
        st6g = sb("st6g", [P, GP, 6])
        mvg = sb("mvg", [P, NB, 2])
        stdg = sb("stdg", [P, NB])
        rstdg = sb("rstdg", [P, NB])
        tg = sb("tg", [P, GP, D])
        x2T = sb("x2T", [P, GP, D])
        n2t = flat(rows, NB * O1, NB, W2)
        o2t = flat(cols, 0, NB, O2)
        in2 = sb("in2", [P, 2, O2])
        in3 = sb("in3", [P, 2, O3])
        in2s = sb("in2s", [P, O2])
        in3s = sb("in3s", [P, O3])
        rid3 = sb("rid3", [P, NB, 3])
        n3t = sb("n3t", [P, 2, W3])
        o3 = sb("o3", [P, 2, O3])
        yt = sb("yt", [P, 2, D])
        ps = ctx.enter_context(nc.psum_tensor("ps", [P, 8 * BANK], F32))
        acc = ps[:, 6 * BANK:6 * BANK + D]
        trn = ps[:, 6 * BANK + D:6 * BANK + 2 * D]
        acc2 = [ps[:, h * BANK:h * BANK + D] for h in range(2)]
        trn2 = ps[:, 2 * BANK:2 * BANK + D]
        threes = [(q, min(3, GP - q)) for q in range(0, GP, 3)]

        def hw_ps(r):
            return ps[:, (6 + r % 2) * BANK:(6 + r % 2) * BANK + D]

        def yps(g):
            return ps[:, 3 * g * BANK:3 * g * BANK + GP * D].rearrange("p (q d) -> p q d", d=D)

        def p2ps(c, m):
            at, w = (6 + c % 2) * BANK, D + 2 * HEADS
            return ps[:, at:at + m * w].rearrange("p (q w) -> p q w", w=w)

        prj = ps[:, 7 * BANK:8 * BANK]

        def two(name):
            return [sem(name + "_a"), sem(name + "_b")]

        s_iota, s_const, s_zero = sem("s_iota"), sem("s_const"), sem("s_zero")
        s_w, s_w2, s_x = sem("s_w"), sem("s_w2"), sem("s_x")
        s_wa, s_wac, s_u, s_uc = sem("s_wa"), sem("s_wac"), sem("s_u"), sem("s_uc")
        s_w2a, s_w2ac, s_was = sem("s_w2a"), sem("s_w2ac"), sem("s_was")
        q_row = [sem(f"q_row{r}") for r in range(4)]
        q_xt = [sem(f"q_xt{r}") for r in range(4)]
        q_z = [sem(f"q_z{r}") for r in range(4)]
        q_neg = [sem(f"q_neg{r}") for r in range(4)]
        q_e = [sem(f"q_e{r}") for r in range(4)]
        q_hw = [sem(f"q_hw{r}") for r in range(4)]
        q_hwc = [sem(f"q_hwc{r}") for r in range(4)]
        q_st = [sem(f"q_st{r}") for r in range(4)]
        s_row, s_col, s_xo, s_ix, s_st1 = two("s_row"), two("s_col"), two("s_xo"), two("s_ix"), two("s_st1")
        s_g, s_prod, s_acc, s_x1, s_hwm, s_y, s_o1 = (two("s_g"), two("s_prod"), two("s_acc"), two("s_x1"), two("s_hwm"),
                                                      two("s_y"), two("s_o1"))
        s_ex, s_c0 = sem("s_ex"), sem("s_c0")
        s_wgt, s_cn = sem("s_wgt"), sem("s_cn")
        s_sc, s_p, s_mv, s_std, s_trn, s_xTb, s_prj = (sem("s_sc"), sem("s_p"), sem("s_mv"), sem("s_std"), sem("s_trn"),
                                                       sem("s_xTb"), sem("s_prj"))
        s_ov, s_pos, s_ovp, s_oh, s_list, s_ids = sem("s_ov"), sem("s_pos"), sem("s_ovp"), sem("s_oh"), sem("s_list"), sem("s_ids")
        s_orow, s_ocol, s_oxo, s_oex, s_scat1 = (sem("s_orow"), sem("s_ocol"), sem("s_oxo"), sem("s_oex"),
                                                        sem("s_scat1"))
        s_yc, s_o1a, s_yT, s_c1, s_mvg, s_sg = (sem("s_yc"), sem("s_o1a"), sem("s_yT"), sem("s_c1"),
                                                       sem("s_mvg"), sem("s_sg"))
        s_x2, s_x2T, s_x2c, s_p2, s_p2c = sem("s_x2"), sem("s_x2T"), sem("s_x2c"), sem("s_p2"), sem("s_p2c")
        s_st2, s_st2o = sem("s_st2"), sem("s_st2o")
        f_sum, f_gelu = two("f_sum"), two("f_gelu")
        s_rest = two("s_rest")
        s_d2 = sem("s_d2")
        s_c2, s_c3, f_nf, f_h = sem("s_c2"), sem("s_c3"), sem("f_nf"), sem("f_h")

        s_bad, s_flag, s_fdone = sem("s_bad"), sem("s_flag"), sem("s_fdone")
        g_w, g_wa, g_wac, g_u, g_uc = sem("g_w"), sem("g_wa"), sem("g_wac"), sem("g_u"), sem("g_uc")
        g_in = {l: sem(f"g_in_{l}") for l in (1, 0, 2, 3)}
        g_dve = {l: sem(f"g_dve_{l}") for l in (1, 0, 2, 3)}
        g_act = {l: sem(f"g_act_{l}") for l in (0, 2, 3)}
        g_pe = {l: sem(f"g_pe_{l}") for l in (0, 2, 3)}
        g_st = {l: sem(f"g_st_{l}") for l in (1, 0, 2, 3)}
        g_rows = {l: sem(f"g_rows_{l}") for l in (0, 2, 3)}
        g_prod = {l: sem(f"g_prod_{l}") for l in (0, 2, 3)}
        g_acc = {l: sem(f"g_acc_{l}") for l in (0, 2, 3)}
        g_sj, g_sum, g_gelu, g_last = sem("g_sj"), sem("g_sum"), sem("g_gelu"), sem("g_last")

        block = ctx.enter_context(nc.Block())
        OVER = (NB, PAIRS, 0)

        def apart(eng, *waits):
            wait_apart(eng, s_const, waits)

        GATHERED = 16 * (KM - 1)

        def past(l, h):
            return l * (PAIRS + 1 - h)

        def past_gathers(l, h):
            return l * (GATHERED * PAIRS + (16 * KO if h == 0 else 0))

        def rows_of(it, h):
            return it * PAIR + h * SECOND

        def own(n, h):
            return P if isinstance(n, int) and n == NB - 1 else OWN[h]

        def all_but_last(eng, body):
            for h in range(2):
                body(h, 0, h, True)
            with eng.Fori(1, PAIRS - 1) as it:
                for h in range(2):
                    body(it * 2 + h, it, h, True)

        def free(eng, semaphore, value):
            if not (isinstance(value, int) and value == 0):
                eng.wait_ge(semaphore, value)

        def pairs(eng, body):
            all_but_last(eng, body)
            for h in range(2):
                body(NB - 2 + h, PAIRS - 1, h, False)

        def first_rows(n, r):
            return cols[:, r, :] if isinstance(n, int) and n < 2 else rows[:, r, 0:N]

        def of_block_before(part, n, it, h):
            if h:
                part(n - 1, it, 0)
            elif not (isinstance(it, int) and it == 0):
                part(n - 1, it - 1, 1)

        def pipelined(eng, front, back):
            def body(n, it, h, more):
                front(n, it, h, more)
                of_block_before(back, n, it, h)
            pairs(eng, body)
            back(NB - 1, PAIRS - 1, 1)

        def quads(eng, body):
            for r in range(4):
                body(r, 0, r, rows_of(r // 2, r % 2))
            with eng.Fori(1, NB // 4) as it:
                for r in range(4):
                    body(it * 4 + r, it, r, it * (2 * PAIR) + rows_of(r // 2, r % 2))
            for r in range(NB % 4):
                body(NB - 2 + r, NB // 4, r, rows_of(PAIRS - 1, r))

        def gathered(h):
            return G[:, h * KM:(h + 1) * KM, :]

        chunks = [(c, min(BANK, N - c)) for c in range(0, N, BANK)]

        def mm(pe, dst, lhsT, rhs, start, stop):
            return pe.matmul(dst, lhsT, rhs, start=start, stop=stop, skip_group_check=True)

        def layer1_io(sp, r):
            for h in range(2):
                sp.dma_start(own1_all[:, h::2, :],
                             bass.AP(own1.tensor, rows_of(0, h) * O1, [[O1, P], [PAIR * O1, PAIRS], [1, O1]])).then_inc(s_o1a, 16)
            for g in range(2):
                sp.wait_ge(s_p2c, 8 * r + 4 * g + 4)
                for t_, table, w, stored in ((n2t, near2, W2, s_st2), (o2t, own2, O2, s_st2o)):
                    for h in range(2):
                        n = g * GP + (g * GP + h) % 2
                        count = len(range(n, (g + 1) * GP, 2))
                        sp.dma_start(bass.AP(table.tensor, rows_of(n // 2, h) * w, [[w, OWN[h]], [PAIR * w, count], [1, w]]),
                                     t_[0:OWN[h], n:(g + 1) * GP:2, :]).then_inc(stored, 16)
                    if g:
                        sp.dma_start(table[N - P + OWN[1]:N, :], t_[OWN[1]:P, NB - 1, :]).then_inc(stored, 16)
            sp.wait_ge(s_st2, 16 * 5 * (r + 1))
            sp.wait_ge(s_st2o, 16 * 5 * (r + 1))

        def layer1_act(act, r):
            for at, m in chunks:
                act.activation(xT_s[:, at:at + m], ps[:, at:at + m], ACT.Copy).then_inc(s_yc, 1)
            for g in range(2):
                act.wait_ge(s_mvg, 2 * r + g + 1)
                act.activation(stdg[:, g * GP:(g + 1) * GP], mvg[:, g * GP:(g + 1) * GP, 1], ACT.Sqrt,
                               bias=eps[:, 0:1]).then_inc(s_sg, 1)
                act.wait_ge(s_x2T, 2 * r + g + 1)
                if g:
                    act.wait_ge(s_p2, 8 * r + 4 * g)
                act.activation(x2T[:, :, :], yps(g), ACT.Copy).then_inc(s_x2c, 1)
                for c, (q, m) in enumerate(threes):
                    act.wait_ge(s_p2, 8 * r + 4 * g + c + 1)
                    src = p2ps(c, m)
                    n = g * GP + q
                    act.activation(n2t[:, n:n + m, :], src[:, :, 0:W2], ACT.Copy)
                    act.activation(o2t[:, n:n + m, D:O2], src[:, :, W2:W2 + HEADS], ACT.Copy).then_inc(s_p2c, 1)

        def layer1_pe(pe, r):
            pe.wait_ge(s_yc, len(chunks) * (r + 1))
            for g in range(2):
                for q in range(GP):
                    n = g * GP + q
                    start = rows_of(n // 2, n % 2)
                    last = pe.transpose(yps(g)[:, q, :], xT_s[:, start:start + P], ident[:, :])
                last.then_inc(s_yT, 1)
            for g in range(2):
                pe.wait_ge(s_x2, 2 * r + g + 1)
                for q in range(GP):
                    last = pe.transpose(yps(g)[:, q, :], o2t[:, g * GP + q, 0:D], ident[:, :])
                last.then_inc(s_x2T, 1)
                pe.wait_ge(s_x2c, 2 * r + g + 1)
                for c, (q, m) in enumerate(threes):
                    if 8 * r + 4 * g + c >= 2:
                        pe.wait_ge(s_p2c, 8 * r + 4 * g + c - 1)
                    for k in range(m):
                        last = mm(pe, p2ps(c, m)[:, k, :], x2T[:, q + k, :], w2c[:, :], True, True)
                    last.then_inc(s_p2, 1)

        def layer1_dve(dve, r):
            c1 = Steps(dve, s_c1)
            c1.base = r * 10
            for g in range(2):
                at = slice(g * GP, (g + 1) * GP)
                dve.wait_ge(s_yT, 2 * r + g + 1)
                dve.wait_ge(s_o1a, 32 * (r + 1))
                if g:
                    dve.wait_ge(s_x2, 2 * r + g)
                c1.done(dve.tensor_tensor(tg[:, :, :], yps(g), own1_all[:, at, D:2 * D], ALU.add))
                c1.done(dve.tensor_tensor(tg[:, :, :], tg[:, :, :], own1_all[:, at, 2 * D:O1].broadcast_to([P, GP, D]), ALU.mult))
                c1.done(dve.scalar_tensor_tensor(out=tg[:, :, :], in0=tg[:, :, :], scalar=0.0, in1=own1_all[:, at, 0:D],
                                                 op0=ALU.max, op1=ALU.add))
                for q in range(GP):
                    last = dve.bn_stats(st6g[:, q, :], tg[:, q, :])
                c1.done(last)
                for q in range(GP):
                    last = dve.bn_aggr(mvg[:, g * GP + q, :], st6g[:, q, :])
                last.then_inc(s_mvg, 1)
                dve.wait_ge(s_sg, 2 * r + g + 1)
                c1.done(dve.reciprocal(rstdg[:, at], stdg[:, at]))
                for q in range(GP):
                    n = g * GP + q
                    last = dve.tensor_scalar(o2t[:, n, 0:D], tg[:, q, :], mvg[:, n, 0:1], rstdg[:, n:n + 1], ALU.subtract,
                                             ALU.mult)
                last.then_inc(s_x2, 1)

            assert c1.count == 10

        TURNS = -(-N // KO)
        TAIL = N - KO * (TURNS - 1)

        def general_if_needed(eng, path):
            eng.wait_ge(s_flag, 1)
            with eng.If(eng.value_load(flag[0:1, 0:1], min_val=0, max_val=1) > 0):
                path(eng)

        def every_block(eng, body):
            with eng.Fori(0, PAIRS) as it:
                for h in range(2):
                    body(it * 2 + h, it, h)

        def every_turn(eng, n, body):
            with eng.Fori(0, TURNS - 1) as c:
                body(n * TURNS + c, c * KO, KO)
            body(n * TURNS + (TURNS - 1), (TURNS - 1) * KO, TAIL)

        DVE0 = dict(scores=10, weights=12, stats=15, normal=19, hw=22)
        DVE2 = dict(mask=2, stats=19, normal=21, table=23)
        DVE3 = dict(nf=1, stats=4, stats2=11, out=13)
        ACT0, ACT2, ACT3 = dict(p=1, std=2, xTb=3), dict(p=HEADS, std=HEADS + 1, xTb=HEADS + 2), dict(aT=1, h=2, std=3, std2=4)
        PE0, PE2, PE3 = dict(trn=1, prj=2, y=3), dict(trn=1, prj=2), dict(prj=1)

        def step(n, steps, name):
            return n * max(steps.values()) + steps[name]

        def head_step(n, hd, k):
            return n * DVE2["table"] + (DVE2["mask"] + 3 * hd + k)

        def general_sp(sp):
            sp.dma_start(a0_s[:, :], a0[D:2 * D, :]).then_inc(g_w, 16)
            sp.dma_start(xT_s[:, :], xT).then_inc(g_w, 16)

            def own_rows(n, it, h, table, src):
                return table[bass.ds(rows_of(it, h), OWN[h]), :], src[0:OWN[h], :]

            def last_two(table, src):
                sp.dma_start(table[N - P + OWN[1]:N, :], src[OWN[1]:P, :]).then_inc(g_last, 16)

            def first(n, it, h):
                sp.dma_start(rows[:, 0, 0:N], adj[bass.ds(rows_of(it, h), P), :]).then_inc(g_in[1], 16)
                apart(sp, (g_dve[1], n * 3 + 3))
                sp.dma_start(*own_rows(n, it, h, epem[0], ee[:, 0:1])).then_inc(g_st[1], 16)
                sp.dma_start(*own_rows(n, it, h, epem[1], ee[:, 1:2])).then_inc(g_st[1], 16)
            every_block(sp, first)
            sp.wait_ge(g_st[1], 32 * NB)
            for c in range(2):
                last_two(epem[c], ee[:, c:c + 1])
            sp.wait_ge(g_last, 32)
            sp.dma_start(u1_b[:, :], epem[0].rearrange("n a -> (n a)").partition_broadcast(P)).then_inc(g_w, 16)
            sp.dma_start(cols[:, 1, :], epem[1].rearrange("n a -> (n a)").partition_broadcast(P)).then_inc(g_w, 16)

            def turns(n, l, table, w):
                def one(m, at, K):
                    sp.dma_start(G[:, 0:K, 0:w], table[bass.ds(at, K), :].partition_broadcast(P)).then_inc(g_rows[l], 16)
                    apart(sp, (g_prod[l], m + 1))
                every_turn(sp, n, one)

            def layer0(n, it, h):
                start = rows_of(it, h)
                sp.dma_start(rows[:, 0, 0:N], adj[bass.ds(start, P), :]).then_inc(g_in[0], 16)
                sp.dma_start(cols[:, 0, :], adjT[bass.ds(start, P), :]).then_inc(g_in[0], 16)
                sp.dma_start(xo[:, 0, :], x[bass.ds(start, P), :]).then_inc(g_in[0], 16)
                turns(n, 0, near0, W0)
                apart(sp, (g_dve[0], step(n, DVE0, "hw")))
                sp.dma_start(*own_rows(n, it, h, own1, o1[:, 0, :])).then_inc(g_st[0], 16)
                apart(sp, (g_pe[0], step(n, PE0, "y")))
            every_block(sp, layer0)
            last_two(own1, o1[:, 0, :])
            sp.wait_ge(g_st[0], 16 * NB)
            sp.wait_ge(g_last, 48)
            layer1_io(sp, 1)
            for c in range(HEADS):
                for h in range(2):
                    sp.dma_start(bass.AP(sj[c].tensor, rows_of(0, h), [[1, OWN[h]], [PAIR, PAIRS], [1, 1]]),
                                 n2t[0:OWN[h], h::2, D + c:D + c + 1], allow_slow_non_contiguous=True).then_inc(g_st[2], 16)
                sp.dma_start(sj[c][N - P + OWN[1]:N, :], n2t[OWN[1]:P, NB - 1, D + c:D + c + 1]).then_inc(g_st[2], 16)
            sp.wait_ge(g_st[2], 16 * 3 * HEADS)

            def layer2(n, it, h):
                start = rows_of(it, h)
                sp.dma_start(cols[:, 0, :], adj[bass.ds(start, P), :]).then_inc(g_in[2], 16)
                sp.dma_start(in2[:, 0, :], own2[bass.ds(start, P), :]).then_inc(g_in[2], 16)
                for c in range(HEADS):
                    sp.dma_start(u1_b[:, :], sj[c].rearrange("n a -> (n a)").partition_broadcast(P)).then_inc(g_sj, 16)
                    apart(sp, (g_dve[2], head_step(n, c, 1)))
                turns(n, 2, near2, W2)
                apart(sp, (g_dve[2], step(n, DVE2, "table")))
                sp.dma_start(*own_rows(n, it, h, near3, n3t[:, 0, :])).then_inc(g_st[2], 16)
                sp.dma_start(*own_rows(n, it, h, own3, o3[:, 0, :])).then_inc(g_st[2], 16)
            every_block(sp, layer2)
            last_two(near3, n3t[:, 0, :])
            last_two(own3, o3[:, 0, :])
            sp.wait_ge(g_st[2], 16 * 3 * HEADS + 32 * NB)
            sp.wait_ge(g_last, 80)

            def layer3(n, it, h):
                start = rows_of(it, h)
                sp.dma_start(rows[:, 0, 0:N], adj[bass.ds(start, P), :]).then_inc(g_in[3], 16)
                sp.dma_start(in3[:, 0, :], own3[bass.ds(start, P), :]).then_inc(g_in[3], 16)
                turns(n, 3, near3, W3)
                apart(sp, (g_dve[3], step(n, DVE3, "out")))
                sp.dma_start(*own_rows(n, it, h, out, yt[:, 0, :])).then_inc(g_st[3], 16)
            every_block(sp, layer3)
            last_two(out, yt[:, 0, :])
            sp.wait_ge(g_st[3], 16 * NB)
            sp.wait_ge(g_last, 96)

        def general_act(act):
            for c, (at, m) in enumerate(chunks):
                act.wait_ge(g_u, c + 1)
                act.activation(cols[:, 1, at:at + m], ps[:, at:at + m], ACT.Copy).then_inc(g_uc, 1)

            def layer0(n, it, h):
                act.wait_ge(g_dve[0], step(n, DVE0, "scores"))
                act.activation(rows[:, 1, 0:N], rows[:, 1, 0:N], ACT.Exp, bias=nmx[:, 0:1], accum_out=Z[:, 0:1]).then_inc(g_act[0], 1)
                act.wait_ge(g_dve[0], step(n, DVE0, "stats"))
                act.activation(std[:, 1:2], dsum[:, :], ACT.Sqrt)
                act.activation(std[:, 0:1], mv[:, 1:2], ACT.Sqrt, bias=eps[:, 0:1]).then_inc(g_act[0], 1)
                act.wait_ge(g_pe[0], step(n, PE0, "trn"))
                act.activation(xTb[:, :], trn, ACT.Copy).then_inc(g_act[0], 1)
            every_block(act, layer0)
            act.wait_ge(g_pe[0], NB * PE0["y"])
            layer1_act(act, 1)

            def layer2(n, it, h):
                for c in range(HEADS):
                    act.wait_ge(g_dve[2], head_step(n, c, 3))
                    act.activation(rows[:, c, 0:N], rows[:, c, 0:N], ACT.Exp, bias=nmx[:, c:c + 1],
                                   accum_out=Z[:, c:c + 1]).then_inc(g_act[2], 1)
                act.wait_ge(g_dve[2], step(n, DVE2, "stats"))
                act.activation(std[:, 0:1], mv[:, 1:2], ACT.Sqrt, bias=eps[:, 0:1]).then_inc(g_act[2], 1)
                act.wait_ge(g_pe[2], step(n, PE2, "trn"))
                act.activation(xTb[:, :], trn, ACT.Copy).then_inc(g_act[2], 1)
            every_block(act, layer2)

            def layer3(n, it, h):
                def gelu(m, at, K):
                    act.wait_ge(g_sum, m + 1)
                    act.activation(prod[:, 0:K, :], prod[:, 0:K, :], ACT.Gelu).then_inc(g_gelu, 1)
                every_turn(act, n, gelu)
                act.wait_ge(g_acc[3], n * TURNS + TURNS)
                act.activation(xTb[:, :], acc, ACT.Copy).then_inc(g_act[3], 1)
                act.wait_ge(g_dve[3], step(n, DVE3, "nf"))
                act.activation(t2[:, :], t[:, :], ACT.Gelu).then_inc(g_act[3], 1)
                for name in ("stats", "stats2"):
                    act.wait_ge(g_dve[3], step(n, DVE3, name))
                    act.activation(std[:, 0:1], mv[:, 1:2], ACT.Sqrt, bias=eps[:, 0:1]).then_inc(g_act[3], 1)
            every_block(act, layer3)

        def general_pe(pe):
            pe.wait_ge(g_w, 32)
            mm(pe, ps[:, 0:1], w0T_s[:, :], a0_s[:, :], True, True).then_inc(g_wa, 1)
            pe.wait_ge(g_wac, 1)
            for at, m in chunks:
                mm(pe, ps[:, at:at + m], wa[:, :], xT_s[:, at:at + m], True, True).then_inc(g_u, 1)
            pe.wait_ge(g_uc, len(chunks))
            for at, m in chunks:
                mm(pe, ps[:, at:at + m], zero[0:1, 0:P], zero[0:1, P:P + m], True, False)

            def sums(n, l, transposed):
                mm(pe, acc, zero[0:1, 0:P], zero[0:1, P:P + D], True, False)

                def one(m, at, K):
                    pe.wait_ge(g_prod[l], m + 1)
                    for k in range(K):
                        a, b = (prod[:, k, :], ident[:, :]) if transposed else (ident[:, :], prod[:, k, :])
                        last = mm(pe, acc, a, b, False, K == TAIL and k == K - 1)
                    last.then_inc(g_acc[l], 1)
                every_turn(pe, n, one)

            def layer0(n, it, h):
                pe.wait_ge(g_dve[0], step(n, DVE0, "weights"))
                sums(n, 0, False)
                pe.wait_ge(g_dve[0], step(n, DVE0, "normal"))
                pe.transpose(trn, o1[:, 0, 0:D], ident[:, :]).then_inc(g_pe[0], 1)
                pe.wait_ge(g_act[0], step(n, ACT0, "xTb"))
                mm(pe, prj[:, 0:D], xTb[:, :], w1T_s[:, :], True, True).then_inc(g_pe[0], 1)
                pe.wait_ge(g_dve[0], step(n, DVE0, "hw"))
                for at, m in chunks:
                    last = mm(pe, ps[:, at:at + m], hwm[:, 0, :], cols[:, 0, at:at + m], False, False)
                last.then_inc(g_pe[0], 1)
            every_block(pe, layer0)
            layer1_pe(pe, 1)

            def layer2(n, it, h):
                pe.wait_ge(g_dve[2], head_step(n, HEADS - 1, 3))
                sums(n, 2, False)
                pe.wait_ge(g_dve[2], step(n, DVE2, "normal"))
                pe.transpose(trn, o3[:, 0, 0:D], ident[:, :]).then_inc(g_pe[2], 1)
                pe.wait_ge(g_act[2], step(n, ACT2, "xTb"))
                mm(pe, prj[:, 0:3 * D], xTb[:, :], w3c[:, :], True, True).then_inc(g_pe[2], 1)
            every_block(pe, layer2)

            def layer3(n, it, h):
                pe.wait_ge(g_in[3], n * 32 + 32)
                sums(n, 3, True)
                pe.wait_ge(g_act[3], step(n, ACT3, "aT"))
                mm(pe, prj[:, 0:D], xTb[:, :], u2T_s[:, :], True, True).then_inc(g_pe[3], 1)
            every_block(pe, layer3)

        def general_dve(dve):
            dve.wait_ge(g_wa, 1)
            g = Steps(dve, g_wac)
            dve.tensor_copy(wa1[:, :], ps[:, 0:1]).then_inc(s_was, 1)
            dve.wait_ge(s_was, 2)
            dve.tensor_scalar(wa[:, :], ones[:, :], wa1[:, 0:1], None, ALU.mult).then_inc(g_wac, 1)
            dve.wait_ge(g_uc, len(chunks))

            e = Steps(dve, g_dve[1], 3, s_const)

            def first(n, it, h):
                e.call(n)
                dve.wait_ge(g_in[1], n * 16 + 16)
                a = rows[:, 0, 0:N]
                for k, (sign, u) in enumerate([(ALU.is_gt, u1_b[:, :]), (ALU.is_lt, cols[:, 1, :]),
                                               (ALU.is_lt, u1_b[:, :]), (ALU.is_gt, cols[:, 1, :])]):
                    last = dve.scalar_tensor_tensor(out=rows[:, k % 2 + 1, 0:N] if k < 2 else rows[:, 3, 0:N] if k == 2 else junk[:, 0:N],
                                                    in0=a, scalar=0.0, in1=u, op0=sign,
                                                    op1=ALU.mult, accum_out=zz[:, k:k + 1])
                e.done(last)
                e.done(dve.tensor_reduce(ez[:, :], zz[:, :].rearrange("p (s k) -> p s k", k=2), AX.X, ALU.add))
                e.done(dve.scalar_tensor_tensor(out=ee[:, :], in0=ez[:, :], scalar=SLOPE, in1=ez[:, :], op0=ALU.mult,
                                                op1=ALU.max))
                dve.wait_ge(g_st[1], n * 32 + 32)
            every_block(dve, first)
            dve.wait_ge(g_w, 64)

            def turns(n, l, product):
                def one(m, at, K):
                    dve.wait_ge(g_rows[l], m * 16 + 16)
                    product(m, at, K).then_inc(g_prod[l], 1)
                    dve.wait_ge(g_acc[l], m + 1)
                every_turn(dve, n, one)

            def stats(steps, src):
                steps.done(dve.bn_stats(st6[:, :], src), True)
                steps.done(dve.bn_aggr(mv[:, :], st6[:, :]))

            d0 = Steps(dve, g_dve[0], DVE0["hw"], s_const)

            def layer0(n, it, h):
                d0.call(n)
                dve.wait_ge(g_in[0], n * 48 + 48)
                a, s, w = rows[:, 0, 0:N], rows[:, 1, 0:N], rows[:, 3, 0:N]
                d0.done(dve.tensor_reduce(dsum[:, :], a, AX.X, ALU.add))
                d0.done(dve.tensor_scalar(st6[:, 0:1], dsum[:, :], 1.0, None, ALU.add))
                d0.done(dve.tensor_scalar(dpos[:, :], st6[:, 0:1], 0.0, None, ALU.is_gt))
                d0.done(dve.tensor_scalar(dsum[:, :], st6[:, 0:1], 1e-34, None, ALU.max))
                d0.done(dve.scalar_tensor_tensor(out=s, in0=a, scalar=0.0, in1=u1_b[:, :], op0=ALU.is_gt, op1=ALU.mult))
                d0.done(dve.scalar_tensor_tensor(out=w, in0=a, scalar=0.0, in1=cols[:, 1, :], op0=ALU.is_lt, op1=ALU.mult))
                d0.done(dve.tensor_tensor(s, s, w, ALU.add))
                d0.done(dve.tensor_scalar(w, a, 0.0, -NEG_INF, ALU.is_equal, ALU.mult))
                d0.done(dve.tensor_tensor(s, s, w, ALU.add))
                d0.done(dve.tensor_reduce(nmx[:, 0:1], s, AX.X, ALU.max, negate=True))
                dve.wait_ge(g_act[0], step(n, ACT0, "p"))
                d0.done(dve.tensor_tensor(w, s, a, ALU.mult))
                d0.done(dve.reciprocal(rz[:, 0:1], Z[:, 0:1]), True)
                turns(n, 0, lambda m, at, K: dve.tensor_tensor(
                    prod[:, 0:K, :], G[:, 0:K, 0:D], rows[:, 3, bass.ds(at, K)].unsqueeze(2).broadcast_to([P, K, D]), ALU.mult))
                d0.done(dve.scalar_tensor_tensor(out=t[:, :], in0=acc, scalar=rz[:, 0:1], in1=xo[:, 0, :], op0=ALU.mult,
                                                 op1=ALU.add))
                stats(d0, t[:, :])
                dve.wait_ge(g_act[0], step(n, ACT0, "std"))
                d0.done(dve.reciprocal(st6[:, 0:1], std[:, 1:2]))
                d0.done(dve.tensor_tensor(o1[:, 0, 2 * D:O1], st6[:, 0:1], dpos[:, :], ALU.mult))
                d0.done(dve.reciprocal(rstd[:, :], std[:, 0:1]))
                d0.done(dve.tensor_scalar(o1[:, 0, 0:D], t[:, :], mv[:, 0:1], rstd[:, 0:1], ALU.subtract, ALU.mult))
                dve.wait_ge(g_pe[0], step(n, PE0, "prj"))
                d0.done(dve.tensor_tensor(t[:, :], prj[:, 0:D], b1_b[:, :], ALU.add))
                d0.done(dve.tensor_scalar(o1[:, 0, D:2 * D], t[:, :], o1[:, 0, 2 * D:O1], None, ALU.mult))
                d0.done(dve.tensor_scalar(hwm[:, 0, :], o1[:, 0, D:2 * D], owned[:, bass.ds(n, 1)], None, ALU.mult))
                dve.wait_ge(g_st[0], n * 16 + 16)
                dve.wait_ge(g_pe[0], step(n, PE0, "y"))
            every_block(dve, layer0)
            layer1_dve(dve, 1)
            dve.wait_ge(g_st[2], 16 * 3 * HEADS)

            d2 = Steps(dve, g_dve[2], DVE2["table"], s_const)

            def layer2(n, it, h):
                d2.call(n)
                dve.wait_ge(g_in[2], n * 32 + 32)
                a, pen = cols[:, 0, :], cols[:, 1, :]
                d2.done(dve.tensor_scalar(a, a, -1.0, 1.0, ALU.mult, ALU.add))
                d2.done(dve.tensor_scalar(pen, a, -1.0e9, None, ALU.mult))
                for c in range(HEADS):
                    dve.wait_ge(g_sj, n * (16 * HEADS) + 16 * (c + 1))
                    d2.done(dve.tensor_scalar(rows[:, c, 0:N], u1_b[:, :], in2[:, 0, D + c:D + c + 1], None, ALU.add))
                    d2.done(dve.scalar_tensor_tensor(out=rows[:, c, 0:N], in0=rows[:, c, 0:N], scalar=HD ** -0.5, in1=pen,
                                                     op0=ALU.mult, op1=ALU.add))
                    d2.done(dve.tensor_reduce(nmx[:, c:c + 1], rows[:, c, 0:N], AX.X, ALU.max, negate=True))
                dve.wait_ge(g_act[2], step(n, ACT2, "p"))
                d2.done(dve.reciprocal(rz[:, 0:HEADS], Z[:, :]), True)
                turns(n, 2, lambda m, at, K: dve.tensor_tensor(
                    prod[:, 0:K, :].rearrange("p k (c d) -> p k c d", c=HEADS),
                    G[:, 0:K, 0:D].rearrange("p k (c d) -> p k c d", c=HEADS),
                    rows[:, :, bass.ds(at, K)].rearrange("p c k -> p k c").unsqueeze(3).broadcast_to([P, K, HEADS, HD]), ALU.mult))
                d2.done(dve.tensor_tensor(t[:, :].rearrange("p (c d) -> p c d", c=HEADS), acc.rearrange("p (c d) -> p c d", c=HEADS),
                                          rz[:, 0:HEADS].unsqueeze(2).broadcast_to([P, HEADS, HD]), ALU.mult))
                d2.done(dve.tensor_tensor(t2[:, :], t[:, :], in2[:, 0, 0:D], ALU.add))
                stats(d2, t2[:, :])
                dve.wait_ge(g_act[2], step(n, ACT2, "std"))
                d2.done(dve.reciprocal(rstd[:, :], std[:, 0:1]))
                d2.done(dve.tensor_scalar(o3[:, 0, 0:D], t2[:, :], mv[:, 0:1], rstd[:, 0:1], ALU.subtract, ALU.mult))
                dve.wait_ge(g_pe[2], step(n, PE2, "prj"))
                d2.done(dve.tensor_copy(n3t[:, 0, :], prj[:, 0:D]))
                d2.done(dve.tensor_tensor(o3[:, 0, D:O3], prj[:, D:O3], b3_b[:, :], ALU.add))
                dve.wait_ge(g_st[2], n * 32 + (16 * 3 * HEADS + 32))
            every_block(dve, layer2)

            d3 = Steps(dve, g_dve[3], DVE3["out"], s_const)

            def layer3(n, it, h):
                d3.call(n)
                apart(dve, (g_in[3], n * 32 + 32))
                mine = in3[:, 0, :]

                def message(m, at, K):
                    dve.tensor_tensor(prod[:, 0:K, :], G[:, 0:K, 0:D], mine[:, D:2 * D].unsqueeze(1).broadcast_to([P, K, D]),
                                      ALU.add).then_inc(g_sum, 1)
                    dve.wait_ge(g_gelu, m + 1)
                    return dve.tensor_tensor(prod[:, 0:K, :], prod[:, 0:K, :],
                                             rows[:, 0, bass.ds(at, K)].unsqueeze(2).broadcast_to([P, K, D]), ALU.mult)
                turns(n, 3, message)
                dve.wait_ge(g_pe[3], step(n, PE3, "prj"))
                d3.done(dve.tensor_tensor(t[:, :], prj[:, 0:D], mine[:, 2 * D:3 * D], ALU.add))
                dve.wait_ge(g_act[3], step(n, ACT3, "h"))
                d3.done(dve.tensor_tensor(t[:, :], t2[:, :], mine[:, 0:D], ALU.add))
                stats(d3, t[:, :])
                dve.wait_ge(g_act[3], step(n, ACT3, "std"))
                d3.done(dve.reciprocal(rstd[:, :], std[:, 0:1]))
                d3.done(dve.tensor_scalar(t[:, :], t[:, :], mv[:, 0:1], rstd[:, 0:1], ALU.subtract, ALU.mult))
                d3.done(dve.tensor_tensor(t[:, :], t[:, :], lnw_b[:, :], ALU.mult))
                d3.done(dve.tensor_tensor(t[:, :], t[:, :], lnb_b[:, :], ALU.add))
                d3.done(dve.tensor_tensor(t[:, :], t[:, :], mine[:, 0:D], ALU.add))
                stats(d3, t[:, :])
                dve.wait_ge(g_act[3], step(n, ACT3, "std2"))
                d3.done(dve.reciprocal(rstd[:, :], std[:, 0:1]))
                d3.done(dve.tensor_scalar(yt[:, 0, :], t[:, :], mv[:, 0:1], rstd[:, 0:1], ALU.subtract, ALU.mult))
                dve.wait_ge(g_st[3], n * 16 + 16)
            every_block(dve, layer3)

        @block.sync
        def _(sp):
            sp.dma_start(w0T_s[:, :], w0T).then_inc(s_w, 16)
            sp.dma_start(a0_s[:, :], a0[0:D, :]).then_inc(s_w, 16)
            sp.dma_start(xT_s[:, :], xT).then_inc(s_x, 16)
            sp.dma_start(w0_s[:, :], w0).then_inc(s_w, 16)

            def first_pass(n, it, r, start):
                apart(sp, (q_z[r], it))
                free(sp, q_neg[r], it)
                sp.dma_start(first_rows(n, r), adj[bass.ds(start, P), :]).then_inc(q_row[r], 16)
                apart(sp, (q_hw[r], it))
                sp.dma_start(xt4[:, r, :], xT[:, bass.ds(start, P)]).then_inc(q_xt[r], 16)
            quads(sp, first_pass)

            sp.wait_ge(s_const, 1)
            for dst, src in [(w1T_s[:, :], w1T), (w2c[:, 0:D], w2), (w2T_s[:, :], w2T), (w3c[:, 0:D], wdT),
                             (w3c[:, D:2 * D], wsT), (w3c[:, 2 * D:3 * D], u1T), (u2T_s[:, :], u2T),
                             (b1_b[:, :], b1.partition_broadcast(P)), (b3_b[:, 0:D], msg_b.partition_broadcast(P)),
                             (b3_b[:, D:2 * D], upd_b.partition_broadcast(P)),
                             (lnw_b[:, :], ln_w.partition_broadcast(P)), (lnb_b[:, :], ln_b.partition_broadcast(P))]:
                sp.dma_start(dst, src).then_inc(s_w2, 16)
            for c in range(2):
                for g in range(HEADS):
                    sp.dma_start(a2_s[HD * g:HD * g + HD, HEADS * c + g:HEADS * c + g + 1],
                                 a2[HD * c:HD * c + HD].rearrange("(d a) -> d a", a=1)).then_inc(s_w2, 16)

            for h in range(2):
                sp.dma_start(Vall[:, h::2, KM - 1:KM],
                             bass.AP(adj.tensor, rows_of(0, h) * (N + 1), [[N + 1, P], [PAIR * (N + 1), PAIRS], [1, 1]]),
                             allow_slow_non_contiguous=True).then_inc(s_w2, 16)

            def own_row(n, it, h, users, users_past, table, width):
                apart(sp, (users[h], it + users_past))
                sp.dma_start(G[:, h * KM + KM - 1, 0:width], table[bass.ds(rows_of(it, h), P), :]).then_inc(s_xo[h], 16)

            for h in range(2):
                sp.wait_ge(q_z[h], NB // 4 + 1)
                sp.wait_ge(q_neg[h], NB // 4 + 1)
                sp.wait_ge(s_ix[h], 1)
            for r in range(4):
                sp.wait_ge(q_st[r], 16 * (6 if r < 2 else 5))

            def store1(start, blocks, h, m):
                apart(sp, (s_hwm[h], blocks))
                sp.dma_start(own1[bass.ds(start, m), :], o1[0:m, h, :]).then_inc(s_st1[h], 16)

            def layer0(n, it, h, more):
                start = rows_of(it, h)
                if more:
                    apart(sp, (s_ix[h], it + 1))
                    sp.dma_start(rows[:, h, 0:N], adj[bass.ds(start + PAIR, P), :]).then_inc(s_row[h], 16)
                own_row(n, it, h, s_prod, 0, near0, W0)
                apart(sp, (s_x1[h], it))
                sp.dma_start(xo[:, h, :], x[bass.ds(start, P), :]).then_inc(s_xo[h], 16)
                if not (isinstance(it, int) and it == 0):
                    store1(start - PAIR, it, h, OWN[h])
                apart(sp, (s_y[h], it))
                sp.dma_start(cols[:, h, :], adjT[bass.ds(start, P), :]).then_inc(s_col[h], 16)
            pairs(sp, layer0)
            for h in range(2):
                store1(rows_of(PAIRS - 1, h), PAIRS, h, own(NB - 2 + h, h))

            sp.wait_ge(s_scat1, 16)
            layer1_io(sp, 0)

            def store2(it, h, m):
                apart(sp, (s_o1[h], it + 1 + past(0, h)))
                sp.dma_start(near3[bass.ds(rows_of(it, h), m), :], n3t[0:m, h, :]).then_inc(s_st1[h], 16)
                sp.dma_start(own3[bass.ds(rows_of(it, h), m), :], o3[0:m, h, :]).then_inc(s_st1[h], 16)

            def layer2(n, it, h, more):
                own_row(n, it, h, s_prod, past(1, h), near2, W2)
                apart(sp, (s_x1[h], it + past(1, h)))
                sp.dma_start(in2[:, h, :], own2[bass.ds(rows_of(it, h), P), :]).then_inc(s_xo[h], 16)
                if not (isinstance(it, int) and it == 0):
                    store2(it - 1, h, OWN[h])
            pairs(sp, layer2)
            for h in range(2):
                store2(PAIRS - 1, h, own(NB - 2 + h, h))

            sp.wait_ge(s_scat1, 16 * 3)

            def store3(it, h, m):
                apart(sp, (s_o1[h], it + 1 + past(1, h)))
                sp.dma_start(out[bass.ds(rows_of(it, h), m), :], yt[0:m, h, :]).then_inc(s_st1[h], 16)

            def layer3(n, it, h, more):
                own_row(n, it, h, f_sum, 0, near3, W3)
                mine = own3[bass.ds(rows_of(it, h), P), :]
                sp.dma_start(in3[:, h, D:2 * D], mine[:, D:2 * D]).then_inc(s_xo[h], 16)
                apart(sp, (s_o1[h], it + past(1, h)))
                sp.dma_start(in3[:, h, :].rearrange("p (k d) -> p k d", d=D)[:, 0::2, :],
                             mine.rearrange("p (k d) -> p k d", d=D)[:, 0::2, :]).then_inc(s_rest[h], 16)
                if not (isinstance(it, int) and it == 0):
                    store3(it - 1, h, OWN[h])
            pairs(sp, layer3)
            for h in range(2):
                store3(PAIRS - 1, h, own(NB - 2 + h, h))
            sp.wait_ge(s_scat1, 16 * 4)
            for h in range(2):
                sp.wait_ge(s_st1[h], 64 * PAIRS)
            general_if_needed(sp, general_sp)

        @block.gpsimd
        def _(pool):
            pool.memset(ident[:, :], 0.0).then_inc(s_iota, 1)
            pool.memset(others[:, :], 1.0).then_inc(s_iota, 1)
            pool.memset(before[:, :], 1.0).then_inc(s_iota, 1)
            pool.iota(counting[:, :], pattern=[[1, P]], base=1, channel_multiplier=0,
                      allow_small_or_imprecise_dtypes=True).then_inc(s_iota, 1)
            pool.iota(row_id[:, :], pattern=[[PAIR, PAIRS], [SECOND, 2]], base=0, channel_multiplier=1,
                      allow_small_or_imprecise_dtypes=True).then_inc(s_iota, 1)
            pool.memset(owned[:, :], 1.0).then_inc(s_iota, 1)
            pool.memset(rows[:, :, N:WIDE], 0.0).then_inc(s_iota, 1)
            pool.wait_ge(s_iota, 7)
            pool.affine_select(out=others[:, :], in_=others[:, :], compare_op=ALU.not_equal, fill=0.0, base=0,
                               pattern=[[-1, P]], channel_multiplier=1).then_inc(s_iota, 1)
            pool.affine_select(out=ident[:, :], in_=ident[:, :], compare_op=ALU.not_equal, fill=1.0, base=0,
                               pattern=[[-1, P]], channel_multiplier=1).then_inc(s_iota, 1)
            pool.affine_select(out=before[:, :], in_=before[:, :], compare_op=ALU.is_gt, fill=0.0, base=0,
                               pattern=[[1, P]], channel_multiplier=-1).then_inc(s_iota, 1)
            for h, blocks in ((0, owned[:, 0:NB:2]), (1, owned[:, 1:NB - 1:2])):
                pool.affine_select(out=blocks, in_=blocks, compare_op=ALU.is_gt, fill=0.0, base=OWN[h],
                                   pattern=[[0, PAIRS - h]], channel_multiplier=-1).then_inc(s_iota, 1)

            def gather(dst, table, index, signal):
                pool.indirect_dma_start(out=dst, out_offset=None, in_=table,
                                        in_offset=bass.IndirectOffsetOnAxis(ap=index, axis=0),
                                        bounds_check=N - 1, oob_is_err=False).then_inc(signal, 16)

            def scatter(table, src, signal):
                pool.indirect_dma_start(out=table, out_offset=bass.IndirectOffsetOnAxis(ap=sid[:, 0:1], axis=0), in_=src,
                                        in_offset=None, bounds_check=N - 1, oob_is_err=False).then_inc(signal, 16)

            def main_gathers(l, free, free_past, table, width):
                def one(n, it, h, more):
                    apart(pool, (s_ix[h], it + 1 + l * PAIRS))
                    apart(pool, (free[h], it + free_past(h)))
                    for k in range(KM - 1):
                        gather(G[:, h * KM + k, 0:width], table[:, :], ix[:, h, k:k + 1], s_g[h])
                return one

            def over_gathers(free, free_past, table, width, listed=()):
                pool.wait_ge(free[0], PAIRS + free_past(0))
                for k in range(KO - 1):
                    if k == KM:
                        pool.wait_ge(free[1], PAIRS + free_past(1))
                    if listed and k % 8 == 0:
                        pool.wait_ge(s_oex, listed[k // 8])
                    gather(G[:, k, 0:width], table[:, :], Io[:, k:k + 1], s_g[0])
                gather(G[:, KO - 1, 0:width], table[:, :], gid[:, 0:1], s_g[0])

            pool.wait_ge(s_u, len(chunks))
            pool.iota(xT_s[:, :], pattern=[[1, N]], base=0, channel_multiplier=0,
                      allow_small_or_imprecise_dtypes=True).then_inc(s_cn, 1)
            for r in range(4):
                pool.wait_ge(q_st[r], 16 * (6 if r < 2 else 5))
            stage = main_gathers(0, s_prod, lambda h: 0, near0, W0)
            all_but_last(pool, stage)
            stage(NB - 2, PAIRS - 1, 0, False)
            stage(NB - 1, PAIRS - 1, 1, False)
            pool.wait_ge(s_ids, 2)
            gather(rows[:, 2, 0:N], adj[:, :], gid[:, 0:1], s_orow)
            gather(rows[:, 3, 0:N], adjT[:, :], gid[:, 0:1], s_ocol)
            gather(xo[:, 2, :], x[:, :], gid[:, 0:1], s_oxo)
            over_gathers(s_prod, lambda h: 0, near0, W0, (6, 9, 11))
            for h in range(2):
                pool.wait_ge(s_st1[h], 16 * PAIRS)
            pool.wait_ge(s_hwm[0], PAIRS + 1)
            scatter(own1[:, :], o1[:, 0, :], s_scat1)

            pool.wait_ge(s_st2, 16 * 5)
            pairs(pool, main_gathers(1, s_prod, lambda h: past(1, h), near2, W2))
            pool.wait_ge(s_st2o, 16 * 5)
            gather(in2s[:, :], own2[:, :], gid[:, 0:1], s_oxo)
            over_gathers(s_prod, lambda h: past(1, h), near2, W2)
            for h in range(2):
                pool.wait_ge(s_st1[h], 48 * PAIRS)
            pool.wait_ge(s_o1[0], PAIRS + 1 + past(0, 0))
            scatter(near3[:, :], n3t[:, 0, :], s_scat1)
            scatter(own3[:, :], o3[:, 0, :], s_scat1)
            pool.wait_ge(s_scat1, 16 * 3)
            pairs(pool, main_gathers(2, f_sum, lambda h: 0, near3, W3))
            gather(in3s[:, :], own3[:, :], gid[:, 0:1], s_oxo)
            over_gathers(f_sum, lambda h: 0, near3, W3)
            for h in range(2):
                pool.wait_ge(s_st1[h], 64 * PAIRS)
            pool.wait_ge(s_o1[0], PAIRS + 1 + past(1, 0))
            scatter(out[:, :], yt[:, 0, :], s_scat1)
            pool.wait_ge(s_scat1, 16 * 4)

        @block.scalar
        def _(act):
            act.wait_ge(s_zero, 1)
            for c, (at, m) in enumerate(chunks):
                act.wait_ge(s_u, c + 1)
                act.activation(u1_b[:, at:at + m], ps[:, at:at + m], ACT.Copy).then_inc(s_uc, 1)

            def first_pass(n, it, r, start):
                act.wait_ge(q_row[r], it * 16 + 16)
                act.activation(junkb[:, :], first_rows(n, r), ACT.Relu, scale=-1.0,
                               accum_out=neg[:, bass.ds(n, 1)]).then_inc(q_neg[r], 1)
                free(act, q_st[r], it * 16)
                act.wait_ge(q_hw[r], it + 1)
                act.activation(hw4[:, r, 0:D], hw_ps(r), ACT.Copy).then_inc(q_hwc[r], 1)
                act.wait_ge(q_hwc[r], it + 1)
                act.wait_ge(q_e[r], it + 1)
                m = own(n, r % 2)
                act.dma_start(near0[bass.ds(start, m), :], hw4[0:m, r, :]).then_inc(q_st[r], 16)
            quads(act, first_pass)

            def projected0(n, it, h):
                act.wait_ge(s_prj, n + 1)
                act.activation(o1[:, h, D:2 * D], prj[:, 0:D], ACT.Copy, scale=o1[:, h, 2 * D:O1])
                free(act, s_y[h], it)
                act.activation(hwm[:, h, :], prj[:, 0:D], ACT.Copy, scale=rok[:, h:h + 1]).then_inc(s_hwm[h], 1)

            def layer0(n, it, h, K):
                act.wait_ge(s_sc, n + 1)
                act.activation(pr[:, 0:K, 0], sc[:, 0, 0:K, 0], ACT.Exp, bias=nmx[:, 0:1], accum_out=Z[:, 0:1]).then_inc(s_p, 1)
                if K == KM:
                    of_block_before(projected0, n, it, h)
                    act.wait_ge(s_wgt, n + 1)
                    free(act, s_acc[h], it)
                    for k in range(h * KM, h * KM + KM):
                        last = act.activation(prod[:, k, :], G[:, k, 0:D], ACT.Copy, scale=wgt[:, k - h * KM:k - h * KM + 1])
                    last.then_inc(s_prod[h], 1)
                act.wait_ge(s_mv, n + 1)
                act.activation(std[:, 1:2], dsum[:, :], ACT.Sqrt, bias=ones[:, 0:1])
                act.activation(std[:, 0:1], mv[:, 1:2], ACT.Sqrt, bias=eps[:, 0:1]).then_inc(s_std, 1)
                act.wait_ge(s_trn, n + 1)
                act.activation(xTb[:, :], trn, ACT.Copy).then_inc(s_xTb, 1)

            pairs(act, lambda n, it, h, more: layer0(n, it, h, KM))
            projected0(NB - 1, PAIRS - 1, 1)
            layer0(*OVER, KO)
            projected0(*OVER)

            act.wait_ge(s_y[0], PAIRS + 1)
            layer1_act(act, 0)

            def front2(n, it, h, K):
                act.wait_ge(s_sc, n + 1 + 1 * (NB + 1))
                act.activation(pr[:, 0:K, :], sc[:, 2, 0:K, :], ACT.Exp).then_inc(s_p, 1)

            def back2(n, it, h):
                act.wait_ge(s_mv, n + 1 + 1 * (NB + 1))
                act.activation(std[:, 0:1], mv[:, 1:2], ACT.Sqrt, bias=eps[:, 0:1]).then_inc(s_std, 1)
                act.wait_ge(s_trn, n + 1 + 1 * (NB + 1))
                act.activation(xTb[:, :], trn2, ACT.Copy).then_inc(s_xTb, 1)
            pipelined(act, lambda n, it, h, more: front2(n, it, h, KM), back2)
            front2(*OVER, KO)
            back2(*OVER)

            def sum3(n, it, h):
                act.wait_ge(s_acc[h], it + 1 + past(2, h))
                act.activation(xTb[:, :], acc2[h], ACT.Copy).then_inc(s_xTb, 1)

            def front3(n, it, h, K):
                if K == KM:
                    of_block_before(sum3, n, it, h)
                act.wait_ge(f_sum[h], it + 1)
                part = prod[:, h * KM:h * KM + K, :]
                act.activation(part, part, ACT.Gelu).then_inc(f_gelu[h], 1)

            def back3(n, it, h):
                if isinstance(n, int) and n >= NB - 1:
                    sum3(n, it, h)
                act.wait_ge(f_nf, n + 1)
                act.activation(t2[:, :], t[:, :], ACT.Gelu).then_inc(f_h, 1)
                for k in range(2):
                    act.wait_ge(s_mv, n * 2 + (k + 1) + 2 * (NB + 1))
                    act.activation(std[:, 0:1], mv[:, 1:2], ACT.Sqrt, bias=eps[:, 0:1]).then_inc(s_std, 1)
            pipelined(act, lambda n, it, h, more: front3(n, it, h, KM), back3)
            front3(*OVER, KO)
            back3(*OVER)
            for h in range(2):
                act.wait_ge(s_st1[h], 64 * PAIRS)
            general_if_needed(act, general_act)

        @block.tensor
        def _(pe):
            pe.wait_ge(s_w, 16 * 3)
            mm(pe, ps[:, 0:1], w0T_s[:, :], a0_s[:, :], True, True).then_inc(s_wa, 1)
            pe.wait_ge(s_wac, 1)
            pe.wait_ge(s_x, 16)
            for at, m in chunks:
                mm(pe, ps[:, at:at + m], wa[:, :], xT_s[:, at:at + m], True, True).then_inc(s_u, 1)

            def first_pass(n, it, r, start):
                pe.wait_ge(q_xt[r], it * 16 + 16)
                free(pe, q_hwc[(r + 2) % 4], it + r // 2)
                mm(pe, hw_ps(r), xt4[:, r, :], w0_s[:, :], True, True).then_inc(q_hw[r], 1)
            quads(pe, first_pass)

            pe.wait_ge(s_w2, 16 * 22)
            pe.wait_ge(q_hwc[1], NB // 4 + 1)
            mm(pe, prj[:, 0:2 * HEADS], w2T_s[:, :], a2_s[:, :], True, True).then_inc(s_w2a, 1)
            pe.wait_ge(s_w2ac, 1)
            mm(pe, prj[:, 8:9], ones[:, :], wa_sum[:, :], True, True).then_inc(s_w2a, 1)
            pe.wait_ge(s_uc, len(chunks))
            pe.wait_ge(s_zero, 1)
            for at, m in chunks:
                mm(pe, ps[:, at:at + m], zero[0:1, 0:P], zero[0:1, P:P + m], True, False)

            def shares(h, K, columns, part):
                for at, m in part:
                    last = mm(pe, ps[:, at:at + m], hwm[:, h, :], columns[:, at:at + m], False, K == KO)
                return last

            HALF = len(chunks) // 2

            def last_shares(n, it, h):
                shares(h, KM, cols[:, h, :], chunks[HALF:]).then_inc(s_y[h], 1)

            def layer0(n, it, h, K, columns):
                pe.wait_ge(s_prod[h], it + 1)
                for k in range(K):
                    last = mm(pe, acc, ident[:, :], prod[:, h * KM + k, :], k == 0, k == K - 1)
                last.then_inc(s_acc[h], 1)
                if K == KM:
                    of_block_before(last_shares, n, it, h)
                pe.wait_ge(s_x1[h], it + 1)
                pe.transpose(trn, o1[:, h, 0:D], ident[:, :]).then_inc(s_trn, 1)
                pe.wait_ge(s_xTb, n + 1)
                mm(pe, prj[:, 0:D], xTb[:, :], w1T_s[:, :], True, False)
                mm(pe, prj[:, 0:D], ones[0:1, :], b1_b[0:1, :], False, True).then_inc(s_prj, 1)
                pe.wait_ge(s_hwm[h], it + 1)
                if K == KM:
                    pe.wait_ge(s_col[h], it * 16 + 16)
                shares(h, K, columns, chunks[:HALF])

            def layer0_main(n, it, h, more):
                layer0(n, it, h, KM, cols[:, h, :])

            all_but_last(pe, layer0_main)
            pe.wait_ge(s_ov, 1)
            mm(pe, prj[:, 0:NB], before[:, :], over[:, :], True, True)
            mm(pe, prj[:, NB:2 * NB], ones[:, :], over[:, :], True, True).then_inc(s_ovp, 1)
            pe.wait_ge(s_oh, 1)
            for n in range(NB):
                last = mm(pe, prj[:, 2 * NB:2 * NB + 3], junk[:, n * P:(n + 1) * P], rid3[:, n, :], n == 0, n == NB - 1)
            last.then_inc(s_list, 1)
            for h in range(2):
                layer0_main(NB - 2 + h, PAIRS - 1, h, False)
            last_shares(NB - 1, PAIRS - 1, 1)
            pe.wait_ge(s_ocol, 16)
            layer0(*OVER, KO, rows[:, 3, :])
            shares(0, KO, rows[:, 3, :], chunks[HALF:]).then_inc(s_y[0], 1)

            layer1_pe(pe, 0)

            def front2(n, it, h, K):
                pe.wait_ge(s_prod[h], it + 1 + past(1, h))
                for k in range(K):
                    last = mm(pe, acc2[h], ident[:, :], prod[:, h * KM + k, :], k == 0, k == K - 1)
                last.then_inc(s_acc[h], 1)

            def back2(n, it, h):
                pe.wait_ge(s_x1[h], it + 1 + past(1, h))
                pe.transpose(trn2, o3[:, h, 0:D], ident[:, :]).then_inc(s_trn, 1)
                pe.wait_ge(s_xTb, n + 1 + 1 * (NB + 1))
                mm(pe, prj[:, 0:3 * D], xTb[:, :], w3c[:, :], True, True).then_inc(s_prj, 1)

            def layer2(n, it, h, K):
                front2(n, it, h, K)
                back2(n, it, h)
            pairs(pe, lambda n, it, h, more: layer2(n, it, h, KM))
            layer2(*OVER, KO)

            def front3(n, it, h, K):
                pe.wait_ge(s_prod[h], it + 1 + past(2, h))
                for k in range(K):
                    last = mm(pe, acc2[h], prod[:, h * KM + k, :], ident[:, :], k == 0, k == K - 1)
                last.then_inc(s_acc[h], 1)

            def back3(n, it, h):
                pe.wait_ge(s_xTb, n + 1 + 2 * (NB + 1))
                mm(pe, prj[:, 0:D], xTb[:, :], u2T_s[:, :], True, True).then_inc(s_prj, 1)

            def layer3(n, it, h, K):
                front3(n, it, h, K)
                back3(n, it, h)
            pairs(pe, lambda n, it, h, more: layer3(n, it, h, KM))
            layer3(*OVER, KO)
            pe.wait_ge(s_bad, 1)
            mm(pe, prj[:, 0:1], ones[:, :], bads[:, :], True, True).then_inc(s_bad, 1)
            general_if_needed(pe, general_pe)

        @block.vector
        def _(dve):
            dve.memset(a2_s[:, :], 0.0).then_inc(s_const, 1)
            dve.memset(ones[:, :], 1.0)
            dve.memset(zero[:, :], 0.0)
            dve.memset(eps[:, :], EPS).then_inc(s_zero, 1)
            dve.wait_ge(s_wa, 1)
            dve.wait_ge(s_zero, 1)
            dve.tensor_copy(wa1[:, :], ps[:, 0:1]).then_inc(s_was, 1)
            dve.wait_ge(s_was, 1)
            dve.tensor_scalar(wa[:, :], ones[:, :], wa1[:, 0:1], None, ALU.mult).then_inc(s_wac, 1)
            dve.wait_ge(s_uc, len(chunks))

            def first_pass(n, it, r, start):
                dve.wait_ge(q_row[r], it * 16 + 16)
                dve.scalar_tensor_tensor(out=junk[:, 0:N], in0=first_rows(n, r), scalar=0.0, in1=u1_b[:, :], op0=ALU.is_gt,
                                         op1=ALU.mult, accum_out=z4[:, r:r + 1]).then_inc(q_z[r], 1)
                dve.wait_ge(q_z[r], it + 1)
                free(dve, q_st[r], it * 16)
                dve.scalar_tensor_tensor(out=hw4[:, r, D:W0], in0=z4[:, r:r + 1], scalar=SLOPE, in1=z4[:, r:r + 1],
                                         op0=ALU.mult, op1=ALU.max).then_inc(q_e[r], 1)
                if isinstance(n, int) and n == 3:
                    dve.wait_ge(s_iota, 12)
                    for h in range(2):
                        dve.wait_ge(q_neg[h], 1)
                        extract(h, 0, h)

            ex = Steps(dve, s_ex, 8, s_const)

            def rows_at(it, h):
                return cols[:, h, :] if isinstance(it, int) and it == 0 else rows[:, h, :]

            def no_own_entry(n, it, h):
                ex.call(n)
                if not (isinstance(it, int) and it == 0):
                    apart(dve, (s_row[h], it * 16))
                own_columns = rows_at(it, h)[:, bass.ds(rows_of(it, h), P)]
                ex.done(dve.tensor_tensor(own_columns, own_columns, others[:, :], ALU.mult), True)

            def segments(src, count, part):
                m = WIDE // count
                for s in part:
                    last = dve.max(cand[:, 8 * s:8 * s + 8], src[:, m * s:min(m * (s + 1), src.shape[1])])
                return last

            def first_segments(n, it, h):
                no_own_entry(n, it, h)
                segments(rows_at(it, h), SEGS, range(SEGS // 2))

            def last_segments(n, it, h):
                ex.done(segments(rows_at(it, h), SEGS, range(SEGS // 2, SEGS)), True)

            def largest(n, it, h):
                ex.done(dve.max(top[:, 0:8], cand[:, 0:SEGS * 8]), True)
                ex.done(dve.match_replace(cand2[:, :], top[:, 0:8], cand[:, 0:SEGS * 8], 0.0), True)
                ex.done(dve.max(top[:, 8:16], cand2[:, :]), True)
                apart(dve, (s_g[h], it * GATHERED))
                dve.max_index(ix[:, h, 0:8], top[:, 0:8], rows_at(it, h))

            def overflow_flags(n, it, h):
                dve.tensor_copy(Vall[:, bass.ds(n, 1), 0:KM - 1].rearrange("p a k -> p (a k)"), top[:, 0:KM - 1])
                dve.scalar_tensor_tensor(out=flags[:, 0:1], in0=top[:, 7:8], scalar=top[:, 8:9], in1=top[:, 7:8],
                                         op0=ALU.is_equal, op1=ALU.mult)
                ex.done(dve.tensor_reduce(flags[:, 2:3], cand[:, 7:SEGS * 8:8], AX.X, ALU.max))
                ex.done(dve.tensor_scalar(flags[:, 3:4], flags[:, 0:1], flags[:, 2:3], top[:, KM - 1:KM], ALU.max, ALU.max))
                ex.done(dve.scalar_tensor_tensor(out=okay[:, bass.ds(n, 1)], in0=flags[:, 3:4], scalar=0.0,
                                                 in1=owned[:, bass.ds(n, 1)], op0=ALU.is_le, op1=ALU.mult), True)

            def seconds(n, it, h):
                dve.max_index(ix[:, h, 8:16], top[:, 8:16], rows_at(it, h)).then_inc(s_ix[h], 1)

            def keep_indices(n, it, h):
                dve.wait_ge(s_ix[h], it + 1)
                dve.tensor_copy(Iall[:, bass.ds(n, 1), :].rearrange("p a k -> p (a k)"), ix[:, h, :])

            def extract(n, it, h):
                for stage in (first_segments, last_segments, largest, overflow_flags, seconds, keep_indices):
                    stage(n, it, h)

            quads(dve, first_pass)

            dve.wait_ge(s_w2a, 1)
            dve.tensor_copy(w2c[:, D:D + 2 * HEADS], prj[:, 0:2 * HEADS])
            dve.tensor_reduce(wa_sum[:, :], prj[:, 0:2 * HEADS], AX.X, ALU.add, apply_absolute_value=True).then_inc(s_w2ac, 1)
            dve.wait_ge(s_w2a, 2)
            dve.tensor_scalar(thr[:, :], prj[:, 8:9], 24 * HD ** -0.5 * 1e-9, 5e-7, ALU.mult, ALU.add)

            def norm_stats(steps, src):
                steps.done(dve.bn_stats(st6[:, :], src), True)
                dve.bn_aggr(mv[:, :], st6[:, :]).then_inc(s_mv, 1)

            c0 = Steps(dve, s_c0, 5, s_const)

            def entries(n, K):
                return Vo[:, 0:K] if K == KO else Vall[:, bass.ds(n, 1), 0:K].rearrange("p a k -> p (a k)")

            def scores0(n, it, h, K):
                c0.call(n)
                V = entries(n, K)
                if K == KM:
                    dve.wait_ge(s_g[h], (it + 1) * GATHERED)
                    dve.wait_ge(s_xo[h], it * 32 + 32)
                else:
                    dve.wait_ge(s_g[h], it * GATHERED + 16 * KO)
                dve.tensor_reduce(dsum[:, :], V, AX.X, ALU.add)
                dve.tensor_scalar(sc[:, 2, 0:K, 0], V, 0.0, -NEG_INF, ALU.is_le, ALU.mult)
                c0.done(dve.scalar_tensor_tensor(out=sc[:, 1, 0:K, 1], in0=V, scalar=0.0, in1=G[:, h * KM:h * KM + K, D],
                                                 op0=ALU.is_gt, op1=ALU.mult))
                c0.done(dve.tensor_tensor(sc[:, 0, 0:K, 0], sc[:, 1, 0:K, 1], sc[:, 2, 0:K, 0], ALU.add))
                dve.tensor_reduce(nmx[:, 0:1], sc[:, 0, 0:K, 0], AX.X, ALU.max, negate=True).then_inc(s_sc, 1)

            def products0(n, it, h, K):
                dve.wait_ge(s_p, n + 1)
                dve.reciprocal(rz[:, 0:1], Z[:, 0:1])
                free(dve, s_prod[1 - h], it + h)
                dve.tensor_tensor(wgt[:, 0:K], pr[:, 0:K, 0], entries(n, K), ALU.mult).then_inc(s_wgt, 1)
                if K == KM:
                    return
                dve.wait_ge(s_wgt, n + 1)
                dve.wait_ge(s_acc[h], it)
                dve.tensor_tensor(prod[:, h * KM:h * KM + K, :], G[:, h * KM:h * KM + K, 0:D],
                                  wgt[:, 0:K].unsqueeze(2).broadcast_to([P, K, D]), ALU.mult).then_inc(s_prod[h], 1)

            def residual0(n, it, h, K):
                dve.wait_ge(s_acc[h], it + 1)
                if K == KO:
                    dve.wait_ge(s_oxo, 16)
                mine = xo[:, h if K == KM else 2, :]
                c0.done(dve.scalar_tensor_tensor(out=t[:, :], in0=acc, scalar=rz[:, 0:1], in1=mine, op0=ALU.mult, op1=ALU.add))
                norm_stats(c0, t[:, :])

            def normal0(n, it, h, K):
                dve.wait_ge(s_std, n + 1)
                dve.wait_ge(s_mv, n + 1)
                free(dve, s_st1[h], it * 16)
                dve.reciprocal(o1[:, h, 2 * D:O1], std[:, 1:2])
                c0.done(dve.reciprocal(rstd[:, :], std[:, 0:1]))
                free(dve, s_hwm[h], it)
                ok = okay[:, bass.ds(n, 1)] if K == KM else found[:, 1:2]
                dve.tensor_tensor(rok[:, h:h + 1], o1[:, h, 2 * D:O1], ok, ALU.mult)
                dve.tensor_scalar(o1[:, h, 0:D], t[:, :], mv[:, 0:1], rstd[:, 0:1], ALU.subtract, ALU.mult).then_inc(s_x1[h], 1)

            dve.wait_ge(s_w2, 16 * 22)

            def layer0(n, it, h, more):
                for step_of_n, steps_ahead in ((scores0, (first_segments,)),
                                               (products0, (last_segments, largest, overflow_flags, seconds)),
                                               (residual0, (keep_indices,)), (normal0, ())):
                    step_of_n(n, it, h, KM)
                    if more:
                        for ahead in steps_ahead:
                            ahead(n + 2, it + 1, h)

            all_but_last(dve, layer0)

            scores0(NB - 2, PAIRS - 1, 0, KM)
            products0(NB - 2, PAIRS - 1, 0, KM)
            dve.tensor_tensor(over[:, :], owned[:, :], okay[:, :], ALU.subtract)
            dve.tensor_copy(rid3[:, :, 0], row_id[:, :])
            dve.tensor_copy(rid3[:, :, 2], Vall[:, :, KM - 1])
            dve.memset(rid3[:, :, 1], 1.0).then_inc(s_ov, 1)
            dve.wait_ge(s_ovp, 1)
            pos = Steps(dve, s_pos)
            pos.done(dve.tensor_copy(psn[:, 0, :], prj[:, NB:2 * NB]))
            pos.done(dve.tensor_tensor_scan(psn[:, 1, :], ones[:, 0:NB], psn[:, 0, :], 0.0, ALU.mult, ALU.add))
            pos.done(dve.tensor_tensor(psn[:, 0, :], psn[:, 1, :], psn[:, 0, :], ALU.subtract))
            pos.done(dve.tensor_tensor(psn[:, 2, :], prj[:, 0:NB], psn[:, 0, :], ALU.add))
            pos.done(dve.scalar_tensor_tensor(out=psn[:, 2, :], in0=psn[:, 2, :], scalar=1.0, in1=over[:, :], op0=ALU.add,
                                              op1=ALU.mult))
            dve.tensor_tensor(junk[:, :].rearrange("p (n c) -> p n c", c=P),
                              psn[:, 2, :].unsqueeze(2).broadcast_to([P, NB, P]),
                              counting[:, :].unsqueeze(1).broadcast_to([P, NB, P]), ALU.is_equal).then_inc(s_oh, 1)
            dve.wait_ge(s_list, 1)
            pos.done(dve.tensor_copy(found[:, :], prj[:, 2 * NB:2 * NB + 3]))
            dve.tensor_copy(gid[:, :], found[:, 0:1]).then_inc(s_ids, 1)
            pos.done(dve.tensor_scalar(sidf[:, :], found[:, 1:2], -2.0 * N, 2.0 * N, ALU.mult, ALU.add))
            dve.tensor_tensor(sid[:, :], sidf[:, :], found[:, 0:1], ALU.add).then_inc(s_ids, 1)

            for stage in (residual0, normal0):
                stage(NB - 2, PAIRS - 1, 0, KM)
            for stage in (scores0, products0):
                stage(NB - 1, PAIRS - 1, 1, KM)
            oex = Steps(dve, s_oex)
            dve.wait_ge(s_orow, 16)
            dve.wait_ge(s_cn, 1)
            oex.done(dve.scalar_tensor_tensor(out=rows[:, 2, 0:N], in0=xT_s[:, :], scalar=found[:, 0:1], in1=rows[:, 2, 0:N],
                                              op0=ALU.not_equal, op1=ALU.mult))
            oex.done(segments(rows[:, 2, :], OSEGS, range(OSEGS)))
            oex.done(dve.tensor_reduce(flags[:, 2:3], cand[:, 7::8], AX.X, ALU.max))
            for stage in (residual0, normal0):
                stage(NB - 1, PAIRS - 1, 1, KM)
            for k in range(KO // 8):
                at = slice(8 * k, 8 * k + 8)
                oex.done(dve.max(Vo[:, at], cand[:, :]))
                if k < KO // 8 - 1:
                    oex.done(dve.match_replace(cand[:, :], Vo[:, at], cand[:, :], 0.0))
                oex.done(dve.max_index(Io[:, at], Vo[:, at], rows[:, 2, :]))
            for k in range(1, KO // 8):
                dve.scalar_tensor_tensor(out=flags[:, k - 1:k], in0=Vo[:, 8 * k - 1:8 * k], scalar=Vo[:, 8 * k:8 * k + 1],
                                         in1=Vo[:, 8 * k - 1:8 * k], op0=ALU.is_equal, op1=ALU.mult)
            oex.done(dve.tensor_copy(flags[:, 3:4], Vo[:, KO - 1:KO]))
            oex.done(dve.tensor_reduce(bad[:, 3:4], flags[:, :], AX.X, ALU.max))
            oex.done(dve.tensor_scalar(bad[:, 3:4], bad[:, 3:4], 0.0, None, ALU.is_gt))
            oex.done(dve.tensor_copy(Vo[:, KO - 1:KO], found[:, 2:3]))
            for stage in (scores0, products0, residual0, normal0):
                if stage is products0:
                    dve.wait_ge(s_acc[1], PAIRS)
                stage(*OVER, KO)
            c0.call(0)

            layer1_dve(dve, 0)

            def copy_indices(n, h):
                dve.tensor_copy(ix[:, h, :], Iall[:, bass.ds(n, 1), :].rearrange("p a k -> p (a k)")).then_inc(s_ix[h], 1)

            c2, d2s = Steps(dve, s_c2, 7, s_const), Steps(dve, s_d2, 4, s_const)

            def own2_of(h, K):
                return in2[:, h, :] if K == KM else in2s[:, :]

            def front2(n, it, h, K, more):
                c2.call(n)
                V = entries(n, K)
                g = G[:, h * KM:h * KM + K, :]
                mine, rzh = own2_of(h, K), rz[:, h * HEADS:(h + 1) * HEADS]
                if K == KM:
                    dve.wait_ge(s_g[h], (it + 1) * GATHERED + past_gathers(1, h))
                    dve.wait_ge(s_xo[h], it * 32 + 32 + 1 * (32 * PAIRS))
                else:
                    dve.wait_ge(s_g[h], it * GATHERED + 16 * KO + past_gathers(1, h))
                    dve.wait_ge(s_oxo, 32)
                if more:
                    copy_indices(n + 2, h)
                c2.done(dve.tensor_scalar(wgt[:, 0:K], V, -1.0, 1.0, ALU.mult, ALU.add))
                c2.done(dve.tensor_scalar(wgt[:, 0:K], wgt[:, 0:K], -1.0e9, None, ALU.mult))
                c2.done(dve.tensor_tensor(sc[:, 0, 0:K, :], g[:, :, D:W2],
                                          mine[:, D:O2].unsqueeze(1).broadcast_to([P, K, HEADS]), ALU.add))
                c2.done(dve.scalar_tensor_tensor(out=sc[:, 1, 0:K, :], in0=sc[:, 0, 0:K, :], scalar=HD ** -0.5,
                                                 in1=wgt[:, 0:K].unsqueeze(2).broadcast_to([P, K, HEADS]), op0=ALU.mult,
                                                 op1=ALU.add))
                c2.done(dve.tensor_reduce(nmx[:, :], sc[:, 1, 0:K, :].rearrange("p k c -> p c k"), AX.X, ALU.max))
                dve.tensor_tensor(sc[:, 2, 0:K, :], sc[:, 1, 0:K, :], nmx[:, :].unsqueeze(1).broadcast_to([P, K, HEADS]),
                                  ALU.subtract).then_inc(s_sc, 1)
                dve.wait_ge(s_p, n + 1 + 1 * (NB + 1))
                dve.wait_ge(s_acc[h], it + past(1, h))
                if K == KO:
                    dve.wait_ge(s_acc[1], PAIRS + past(1, 1))
                dve.tensor_tensor(prod[:, h * KM:h * KM + K, :].rearrange("p k (c d) -> p k c d", c=HEADS),
                                  g[:, :, 0:D].rearrange("p k (c d) -> p k c d", c=HEADS),
                                  pr[:, 0:K, :].unsqueeze(3).broadcast_to([P, K, HEADS, HD]), ALU.mult).then_inc(s_prod[h], 1)
                c2.done(dve.tensor_reduce(Z[:, :], pr[:, 0:K, :].rearrange("p k c -> p c k"), AX.X, ALU.add))
                c2.done(dve.reciprocal(rzh, Z[:, :]))

            def back2(n, it, h, K=KM):
                d2s.call(n)
                mine, rzh = own2_of(h, K), rz[:, h * HEADS:(h + 1) * HEADS]
                dve.wait_ge(s_acc[h], it + 1 + past(1, h))
                d2s.done(dve.tensor_tensor(t[:, :].rearrange("p (c d) -> p c d", c=HEADS),
                                           acc2[h].rearrange("p (c d) -> p c d", c=HEADS),
                                           rzh.unsqueeze(2).broadcast_to([P, HEADS, HD]), ALU.mult))
                d2s.done(dve.tensor_tensor(t2[:, :], t[:, :], mine[:, 0:D], ALU.add))
                norm_stats(d2s, t2[:, :])
                dve.wait_ge(s_std, n + 1 + 1 * (NB + 1))
                dve.wait_ge(s_mv, n + 1 + 1 * (NB + 1))
                dve.wait_ge(s_st1[h], it * 32 + 16 * PAIRS)
                d2s.done(dve.reciprocal(rstd[:, :], std[:, 0:1]))
                dve.tensor_scalar(o3[:, h, 0:D], t2[:, :], mv[:, 0:1], rstd[:, 0:1], ALU.subtract, ALU.mult).then_inc(s_x1[h], 1)
                dve.wait_ge(s_prj, n + 1 + 1 * (NB + 1))
                dve.tensor_copy(n3t[:, h, :], prj[:, 0:D])
                dve.tensor_tensor(o3[:, h, D:O3], prj[:, D:O3], b3_b[:, :], ALU.add).then_inc(s_o1[h], 1)

            for h in range(2):
                copy_indices(h, h)
            pipelined(dve, lambda n, it, h, more: front2(n, it, h, KM, more), back2)
            front2(*OVER, KO, False)
            back2(*OVER, KO)
            c2.call(0)
            d2s.call(0)

            c3 = Steps(dve, s_c3, 9, s_const)

            def own3_of(h, K):
                return in3[:, h, :] if K == KM else in3s[:, :]

            def front3(n, it, h, K, more):
                V = entries(n, K)
                mine = own3_of(h, K)
                part = prod[:, h * KM:h * KM + K, :]
                if K == KM:
                    dve.wait_ge(s_g[h], (it + 1) * GATHERED + past_gathers(2, h))
                    dve.wait_ge(s_xo[h], it * 32 + 32 + 2 * (32 * PAIRS))
                else:
                    dve.wait_ge(s_g[h], it * GATHERED + 16 * KO + past_gathers(2, h))
                    dve.wait_ge(s_oxo, 48)
                    dve.wait_ge(s_acc[1], PAIRS + past(2, 1))
                if more:
                    copy_indices(n + 2, h)
                dve.wait_ge(s_acc[h], it + past(2, h))
                dve.tensor_tensor(part, G[:, h * KM:h * KM + K, 0:D],
                                  mine[:, D:2 * D].unsqueeze(1).broadcast_to([P, K, D]), ALU.add).then_inc(f_sum[h], 1)
                dve.wait_ge(f_gelu[h], it + 1)
                dve.tensor_tensor(part, part, V.unsqueeze(2).broadcast_to([P, K, D]), ALU.mult).then_inc(s_prod[h], 1)

            def back3(n, it, h, K=KM):
                c3.call(n)
                mine = own3_of(h, K)
                dve.wait_ge(s_o1[1 - h], it + h + past(1, 1 - h))
                if K == KM:
                    dve.wait_ge(s_rest[h], it * 16 + 16)
                dve.wait_ge(s_prj, n + 1 + 2 * (NB + 1))
                dve.tensor_tensor(t[:, :], prj[:, 0:D], mine[:, 2 * D:3 * D], ALU.add).then_inc(f_nf, 1)
                dve.wait_ge(f_h, n + 1)
                c3.done(dve.tensor_tensor(t[:, :], t2[:, :], mine[:, 0:D], ALU.add))
                norm_stats(c3, t[:, :])
                dve.wait_ge(s_mv, n * 2 + 1 + 2 * (NB + 1))
                dve.wait_ge(s_std, n * 2 + 1 + 2 * (NB + 1))
                c3.done(dve.reciprocal(rstd[:, :], std[:, 0:1]))
                c3.done(dve.tensor_scalar(t[:, :], t[:, :], mv[:, 0:1], rstd[:, 0:1], ALU.subtract, ALU.mult))
                c3.done(dve.tensor_tensor(t[:, :], t[:, :], lnw_b[:, :], ALU.mult))
                c3.done(dve.tensor_tensor(t[:, :], t[:, :], lnb_b[:, :], ALU.add))
                c3.done(dve.tensor_tensor(t[:, :], t[:, :], mine[:, 0:D], ALU.add))
                norm_stats(c3, t[:, :])
                dve.wait_ge(s_mv, n * 2 + 2 + 2 * (NB + 1))
                dve.wait_ge(s_std, n * 2 + 2 + 2 * (NB + 1))
                dve.wait_ge(s_st1[h], it * 16 + 48 * PAIRS)
                c3.done(dve.reciprocal(rstd[:, :], std[:, 0:1]))
                dve.tensor_scalar(yt[:, h, :], t[:, :], mv[:, 0:1], rstd[:, 0:1], ALU.subtract, ALU.mult).then_inc(s_o1[h], 1)

            dve.wait_ge(s_g[0], past_gathers(2, 0))
            for h in range(2):
                copy_indices(h, h)
            pipelined(dve, lambda n, it, h, more: front3(n, it, h, KM, more), back3)
            front3(*OVER, KO, False)
            back3(*OVER, KO)
            c3.call(0)

            f = Steps(dve, s_fdone)
            dve.wait_ge(q_neg[0], NB // 4 + 1)
            dve.wait_ge(q_neg[1], NB // 4 + 1)
            dve.wait_ge(q_neg[2], NB // 4)
            dve.wait_ge(q_neg[3], NB // 4)
            f.done(dve.tensor_reduce(st6[:, 0:1], neg[:, :], AX.X, ALU.add))
            f.done(dve.tensor_tensor(rstdg[:, :], Vall[:, :, 0], Vall[:, :, KM - 1], ALU.max))
            f.done(dve.tensor_reduce(st6[:, 1:2], rstdg[:, :], AX.X, ALU.min))
            f.done(dve.tensor_scalar(bad[:, 0:1], st6[:, 0:1], 0.0, None, ALU.is_gt))
            f.done(dve.tensor_tensor(bad[:, 1:2], st6[:, 1:2], thr[:, :], ALU.is_le))
            f.done(dve.tensor_scalar(bad[:, 2:3], psn[:, 1, NB - 1:NB], float(P), None, ALU.is_gt))
            dve.tensor_reduce(bads[:, :], bad[:, :], AX.X, ALU.add).then_inc(s_bad, 1)
            dve.wait_ge(s_bad, 2)
            f.done(dve.tensor_scalar(st6[:, 2:3], prj[:, 0:1], 0.5, None, ALU.is_gt))
            dve.tensor_copy(flag[:, :], st6[:, 2:3]).then_inc(s_flag, 1)
            general_if_needed(dve, general_dve)


def kernel(**inputs):
    import numpy as _np
    import concourse.bacc as _bacc
    from concourse import mybir as _mybir
    from concourse.bass_utils import run_bass_kernel_spmd as _run

    a = {k: _np.asarray(v) for k, v in inputs.items()}
    D = a["x"].shape[1]
    laid = {
        "x": a["x"], "xT": a["x"].T, "adj": a["adj"], "adjT": a["adj"].T,
        "w0": a["L0_gnn_W"], "w0T": a["L0_gnn_W"].T, "a0": a["L0_gnn_a"],
        "w1T": a["L1_gnn_W"].T, "b1": a["L1_gnn_b"],
        "w2": a["L2_gnn_W"], "w2T": a["L2_gnn_W"].T, "a2": a["L2_gnn_a"],
        "wsT": a["L3_gnn_msg_w"][:, :D].T, "wdT": a["L3_gnn_msg_w"][:, D:].T, "msg_b": a["L3_gnn_msg_b"],
        "u1T": a["L3_gnn_upd_w"][:, :D].T, "u2T": a["L3_gnn_upd_w"][:, D:].T, "upd_b": a["L3_gnn_upd_b"],
        "ln_w": a["L3_gnn_ln_w"], "ln_b": a["L3_gnn_ln_b"],
    }
    nc = _bacc.Bacc("TRN2", target_bir_lowering=False, num_devices=1)
    arrays, args = {}, {}
    for name, value in laid.items():
        v = _np.ascontiguousarray(value)
        arrays[f"in_{name}_dram"] = v
        args[name] = nc.dram_tensor(f"in_{name}_dram", v.shape, _mybir.dt.from_np(v.dtype), kind="ExternalInput").ap()
    args["out"] = nc.dram_tensor("out_0_dram", a["x"].shape, _mybir.dt.float32, kind="ExternalOutput").ap()
    build(nc, **args)
    r = _run(nc, [arrays], core_ids=[0])
    return r.results[0]["out_0_dram"]
```
